# Optimizing a Trainium2 kernel written in Bass

```python
import numpy as np
import jax
import jax.numpy as jnp

def _softmax(x, axis=-1):
    return jax.nn.softmax(x, axis=axis)

def _gelu(x):
    return jax.nn.gelu(x, approximate=True)

def _silu(x):
    return jax.nn.silu(x)

def _sigmoid(x):
    return jax.nn.sigmoid(x)

def _layernorm(x, axis=-1, eps=1e-05):
    m = jnp.mean(x, axis=axis, keepdims=True)
    v = jnp.var(x, axis=axis, keepdims=True)
    return (x - m) / jnp.sqrt(v + eps)

def _scatter_add(tgt, idx, src, axis=0):
    return tgt.at[idx].add(src)

def _segment_sum(src, seg, n):
    return jax.ops.segment_sum(src, seg, n)
kernel_name = 'mk_gps_d2_gnn_r8_309ef2'

def setup_inputs(seed: int=0):
    np.random.seed(seed)
    _w = jnp.asarray

    def _rec_inputs():
        import jax
        import jax.numpy as jnp
        _gk = jax.random.key(seed)
        x = -0.0003019 + 1 * jax.random.normal(jax.random.fold_in(_gk, 1), (1250, 1024), jnp.float32)
        src = jax.random.randint(jax.random.fold_in(_gk, 2), (20000,), 0, 1250, jnp.int32)
        dst = jnp.minimum((1250 * jax.random.uniform(jax.random.fold_in(_gk, 3), (20000,)) ** 2.0).astype(jnp.int32), 9999)
        _o = jnp.argsort(dst, stable=True)
        src = src[_o]
        dst = dst[_o]
        edge_type_2 = jax.random.randint(jax.random.fold_in(_gk, 12), (20000,), 0, 2, jnp.int32)
        return (x, src, dst, edge_type_2)
    x, src, dst, edge_type_2 = _rec_inputs()

    def _L0_gnn_setup():
        import jax, jax.numpy as jnp
        import numpy as np
        N = 2500
        E = 40000
        D_IN = 1024
        D_OUT = 1024
        key = jax.random.key(seed)
        k1, k2, k3, k4 = jax.random.split(key, 4)
        x = jax.random.normal(k1, (N, D_IN), dtype=jnp.float32)
        edge_index = jax.random.randint(k2, (2, E), 0, N, dtype=jnp.int64)
        W = jax.random.normal(k3, (D_OUT, D_IN), dtype=jnp.float32) * (1.0 / np.sqrt(D_IN))
        b = jax.random.normal(k4, (D_OUT,), dtype=jnp.float32) * 0.01
        return {'x': x, 'edge_index': edge_index, 'W': W, 'b': b}
    _L0_gnn_all = _L0_gnn_setup()
    _L0_gnn_in = {k: v for k, v in _L0_gnn_all.items() if k in ('W', 'b')}
    del _L0_gnn_all

    def _L0_mix_setup():
        import jax, jax.numpy as jnp
        import numpy as np
        DIM = 1024
        HEADS = 16
        DIM_HEAD = 64
        INNER = HEADS * DIM_HEAD
        SCALE = DIM_HEAD ** (-0.5)
        EPS = 1e-05
        key = jax.random.key(seed)
        ks = jax.random.split(key, 5)
        x = jax.random.normal(ks[0], (2, 256, DIM), dtype=jnp.float32)
        W_qkv = jax.random.normal(ks[1], (DIM, 3 * INNER), dtype=jnp.float32) / np.sqrt(DIM)
        gamma = jnp.ones((INNER,), dtype=jnp.float32)
        beta = jnp.zeros((INNER,), dtype=jnp.float32)
        W_out = jax.random.normal(ks[2], (INNER, DIM), dtype=jnp.float32) / np.sqrt(INNER)
        b_out = jnp.zeros((DIM,), dtype=jnp.float32)
        return {'x': x, 'W_qkv': W_qkv, 'gamma': gamma, 'beta': beta, 'W_out': W_out, 'b_out': b_out}
    _L0_mix_all = _L0_mix_setup()
    _L0_mix_in = {k: v for k, v in _L0_mix_all.items() if k in ('W_qkv', 'gamma', 'beta', 'W_out', 'b_out')}
    del _L0_mix_all

    def _L0_ffn_setup():
        import jax, jax.numpy as jnp
        import numpy as np
        DIM = 1024
        HIDDEN = 384
        SCALE = 1.0 / 127.0

        def _dequant(w_int, dtype):
            return w_int.astype(dtype) * jnp.asarray(SCALE, dtype)
        key = jax.random.key(seed)
        k_x, k_g, k_u, k_d = jax.random.split(key, 4)
        x = jax.random.normal(k_x, (4, 256, DIM), dtype=jnp.float32)
        w_gate = jax.random.randint(k_g, (HIDDEN, DIM), -127, 128, dtype=jnp.int32)
        w_up = jax.random.randint(k_u, (HIDDEN, DIM), -127, 128, dtype=jnp.int32)
        w_down = jax.random.randint(k_d, (DIM, HIDDEN), -127, 128, dtype=jnp.int32)
        return {'x': x, 'w_gate': w_gate, 'w_up': w_up, 'w_down': w_down}
    _L0_ffn_all = _L0_ffn_setup()
    _L0_ffn_in = {k: v for k, v in _L0_ffn_all.items() if k in ('w_gate', 'w_up', 'w_down')}
    del _L0_ffn_all

    def _L1_gnn_setup():
        import jax, jax.numpy as jnp
        import numpy as np
        D_MODEL = 1024
        D_FF = 286
        NUM_REL = 2
        EPS = 1e-06

        def t5_layer_norm(x, weight):
            var = jnp.mean(jnp.square(x.astype(jnp.float32)), axis=-1, keepdims=True)
            return weight * (x * jax.lax.rsqrt(var + EPS))

        def rgcn_conv(x, edge_index, edge_type, W_rel, W_root, bias):
            N = x.shape[0]
            src, dst = (edge_index[0], edge_index[1])
            h_src = x[src]
            out = x @ W_root + bias
            for r in range(NUM_REL):
                w = (edge_type == r).astype(x.dtype)
                msg = h_src @ W_rel[r] * w[:, None]
                sums = jax.ops.segment_sum(msg, dst, num_segments=N)
                cnt = jax.ops.segment_sum(w, dst, num_segments=N)
                out = out + sums / jnp.maximum(cnt, 1.0)[:, None]
            return out
        key = jax.random.key(seed)
        ks = jax.random.split(key, 8)
        N, E = (2500, 40000)
        hidden_states = jax.random.normal(ks[0], (N, D_MODEL), dtype=jnp.float32)
        edge_index = jax.random.randint(ks[1], (2, E), 0, N, dtype=jnp.int64)
        edge_type = jax.random.randint(ks[2], (E,), 0, NUM_REL, dtype=jnp.int64)
        ln_weight = jnp.ones((D_MODEL,), dtype=jnp.float32)
        W_rel = jax.random.normal(ks[3], (NUM_REL, D_MODEL, D_FF), dtype=jnp.float32) * (1.0 / np.sqrt(D_MODEL))
        W_root = jax.random.normal(ks[4], (D_MODEL, D_FF), dtype=jnp.float32) * (1.0 / np.sqrt(D_MODEL))
        conv_bias = jnp.zeros((D_FF,), dtype=jnp.float32)
        wo_weight = jax.random.normal(ks[5], (D_FF, D_MODEL), dtype=jnp.float32) * (1.0 / np.sqrt(D_FF))
        return {'hidden_states': hidden_states, 'edge_index': edge_index, 'edge_type': edge_type, 'ln_weight': ln_weight, 'W_rel': W_rel, 'W_root': W_root, 'conv_bias': conv_bias, 'wo_weight': wo_weight}
    _L1_gnn_all = _L1_gnn_setup()
    _L1_gnn_in = {k: v for k, v in _L1_gnn_all.items() if k in ('ln_weight', 'W_rel', 'W_root', 'conv_bias', 'wo_weight')}
    del _L1_gnn_all

    def _L1_mix_setup():
        import jax, jax.numpy as jnp
        import numpy as np
        B, N, D, H = (4, 512, 1024, 16)
        HD = D // H

        def _kernel(x):
            return jax.nn.elu(x) + 1.0
        key = jax.random.key(seed)
        k1, k2, k3, k4 = jax.random.split(key, 4)
        x = jax.random.normal(k1, (B, N, D), dtype=jnp.float32)
        w_qkv = jax.random.normal(k2, (3 * D, D), dtype=jnp.float32) * (1.0 / np.sqrt(D))
        w_out = jax.random.normal(k3, (D, D), dtype=jnp.float32) * (1.0 / np.sqrt(D))
        b_out = jax.random.normal(k4, (D,), dtype=jnp.float32) * 0.01
        return {'x': x, 'w_qkv': w_qkv, 'w_out': w_out, 'b_out': b_out}
    _L1_mix_all = _L1_mix_setup()
    _L1_mix_in = {k: v for k, v in _L1_mix_all.items() if k in ('w_qkv', 'w_out', 'b_out')}
    del _L1_mix_all

    def _L1_ffn_setup():
        import jax, jax.numpy as jnp
        import numpy as np
        E = 8
        D = 1024
        H = 256
        TOP_K = 2
        key = jax.random.key(seed)
        k_x, k_g, k_w1, k_w2 = jax.random.split(key, 4)
        B, S = (4, 256)
        inp = {'input': jax.random.normal(k_x, (B, S, D), dtype=jnp.float32), 'Wg': jax.random.normal(k_g, (D, E), dtype=jnp.float32) * 0.02, 'W1': jax.random.normal(k_w1, (E, D, H), dtype=jnp.float32) * 0.02, 'b1': jnp.zeros((E, H), dtype=jnp.float32), 'W2': jax.random.normal(k_w2, (E, H, D), dtype=jnp.float32) * 0.02, 'b2': jnp.zeros((E, D), dtype=jnp.float32)}
        return inp
    _L1_ffn_all = _L1_ffn_setup()
    _L1_ffn_in = {k: v for k, v in _L1_ffn_all.items() if k in ('Wg', 'W1', 'b1', 'W2', 'b2')}
    del _L1_ffn_all
    return {'x': x, 'src': src, 'dst': dst, 'edge_type_2': edge_type_2, 'L0_gnn_W': _L0_gnn_in['W'], 'L0_gnn_b': _L0_gnn_in['b'], 'L0_mix_W_qkv': _L0_mix_in['W_qkv'], 'L0_mix_gamma': _L0_mix_in['gamma'], 'L0_mix_beta': _L0_mix_in['beta'], 'L0_mix_W_out': _L0_mix_in['W_out'], 'L0_mix_b_out': _L0_mix_in['b_out'], 'L0_ffn_w_gate': _L0_ffn_in['w_gate'], 'L0_ffn_w_up': _L0_ffn_in['w_up'], 'L0_ffn_w_down': _L0_ffn_in['w_down'], 'L1_gnn_ln_weight': _L1_gnn_in['ln_weight'], 'L1_gnn_W_rel': _L1_gnn_in['W_rel'], 'L1_gnn_W_root': _L1_gnn_in['W_root'], 'L1_gnn_conv_bias': _L1_gnn_in['conv_bias'], 'L1_gnn_wo_weight': _L1_gnn_in['wo_weight'], 'L1_mix_w_qkv': _L1_mix_in['w_qkv'], 'L1_mix_w_out': _L1_mix_in['w_out'], 'L1_mix_b_out': _L1_mix_in['b_out'], 'L1_ffn_Wg': _L1_ffn_in['Wg'], 'L1_ffn_W1': _L1_ffn_in['W1'], 'L1_ffn_b1': _L1_ffn_in['b1'], 'L1_ffn_W2': _L1_ffn_in['W2'], 'L1_ffn_b2': _L1_ffn_in['b2']}

def reference(x, src, dst, edge_type_2, L0_gnn_W, L0_gnn_b, L0_mix_W_qkv, L0_mix_gamma, L0_mix_beta, L0_mix_W_out, L0_mix_b_out, L0_ffn_w_gate, L0_ffn_w_up, L0_ffn_w_down, L1_gnn_ln_weight, L1_gnn_W_rel, L1_gnn_W_root, L1_gnn_conv_bias, L1_gnn_wo_weight, L1_mix_w_qkv, L1_mix_w_out, L1_mix_b_out, L1_ffn_Wg, L1_ffn_W1, L1_ffn_b1, L1_ffn_W2, L1_ffn_b2):
    import jax
    import jax.numpy as jnp

    def _L0_gnn_ref(x, edge_index, W, b):
        import jax, jax.numpy as jnp
        import numpy as np
        N = 2500
        E = 40000
        D_IN = 1024
        D_OUT = 1024
        num_nodes = x.shape[0]
        self_idx = jnp.arange(num_nodes, dtype=edge_index.dtype)
        ei = jnp.concatenate([edge_index, jnp.stack([self_idx, self_idx], axis=0)], axis=1)
        row, col = (ei[0], ei[1])
        h = jnp.einsum('nd,od->no', x, W) + b
        deg = jnp.zeros((num_nodes,), dtype=h.dtype).at[row].add(1.0)
        deg_inv_sqrt = deg ** (-0.5)
        norm = deg_inv_sqrt[row] * deg_inv_sqrt[col]
        msg = norm[:, None] * h[col]
        out = jax.ops.segment_sum(msg, row, num_segments=num_nodes)
        return out

    def _L0_mix_ref(x, W_qkv, gamma, beta, W_out, b_out):
        import jax, jax.numpy as jnp
        import numpy as np
        DIM = 1024
        HEADS = 16
        DIM_HEAD = 64
        INNER = HEADS * DIM_HEAD
        SCALE = DIM_HEAD ** (-0.5)
        EPS = 1e-05
        b, n, _ = x.shape
        qkv = x @ W_qkv
        q, k, v = jnp.split(qkv, 3, axis=-1)

        def split_heads(t):
            return t.reshape(b, n, HEADS, DIM_HEAD).transpose(0, 2, 1, 3)
        q, k, v = (split_heads(q), split_heads(k), split_heads(v))
        dots = jnp.einsum('bhid,bhjd->bhij', q, k) * SCALE
        attn = jax.nn.relu(dots)
        out = jnp.einsum('bhij,bhjd->bhid', attn, v)
        out = out.transpose(0, 2, 1, 3).reshape(b, n, INNER)
        mu = jnp.mean(out, axis=-1, keepdims=True)
        var = jnp.mean(jnp.square(out - mu), axis=-1, keepdims=True)
        normed = (out - mu) / jnp.sqrt(var + EPS) * gamma + beta
        return normed @ W_out + b_out

    def _L0_ffn_ref(x, w_gate, w_up, w_down):
        import jax, jax.numpy as jnp
        import numpy as np
        DIM = 1024
        HIDDEN = 384
        SCALE = 1.0 / 127.0

        def _dequant(w_int, dtype):
            return w_int.astype(dtype) * jnp.asarray(SCALE, dtype)
        wg = _dequant(w_gate, x.dtype)
        wu = _dequant(w_up, x.dtype)
        wd = _dequant(w_down, x.dtype)
        gate = jnp.einsum('bsd,hd->bsh', x, wg)
        up = jnp.einsum('bsd,hd->bsh', x, wu)
        h = jax.nn.silu(gate) * up
        return jnp.einsum('bsh,dh->bsd', h, wd)

    def _L1_gnn_ref(hidden_states, edge_index, edge_type, ln_weight, W_rel, W_root, conv_bias, wo_weight):
        import jax, jax.numpy as jnp
        import numpy as np
        D_MODEL = 1024
        D_FF = 286
        NUM_REL = 2
        EPS = 1e-06

        def t5_layer_norm(x, weight):
            var = jnp.mean(jnp.square(x.astype(jnp.float32)), axis=-1, keepdims=True)
            return weight * (x * jax.lax.rsqrt(var + EPS))

        def rgcn_conv(x, edge_index, edge_type, W_rel, W_root, bias):
            N = x.shape[0]
            src, dst = (edge_index[0], edge_index[1])
            h_src = x[src]
            out = x @ W_root + bias
            for r in range(NUM_REL):
                w = (edge_type == r).astype(x.dtype)
                msg = h_src @ W_rel[r] * w[:, None]
                sums = jax.ops.segment_sum(msg, dst, num_segments=N)
                cnt = jax.ops.segment_sum(w, dst, num_segments=N)
                out = out + sums / jnp.maximum(cnt, 1.0)[:, None]
            return out
        norm_x = t5_layer_norm(hidden_states, ln_weight)
        y = jax.nn.elu(rgcn_conv(norm_x, edge_index, edge_type, W_rel, W_root, conv_bias))
        y = y @ wo_weight
        return hidden_states + y

    def _L1_mix_ref(x, w_qkv, w_out, b_out):
        import jax, jax.numpy as jnp
        import numpy as np
        B, N, D, H = (4, 512, 1024, 16)
        HD = D // H

        def _kernel(x):
            return jax.nn.elu(x) + 1.0
        b, n, d = x.shape
        qkv = x @ w_qkv.T
        qkv = qkv.reshape(b, n, 3, H, HD)
        q, k, v = (qkv[:, :, 0], qkv[:, :, 1], qkv[:, :, 2])
        q = _kernel(q)
        k = _kernel(k)
        kv = jnp.einsum('bnhd,bnhm->bhdm', k, v)
        z = 1.0 / (jnp.einsum('bnhd,bhd->bnh', q, k.sum(axis=1)) + 1e-06)
        out = jnp.einsum('bnhd,bhdm,bnh->bnhm', q, kv, z)
        out = out.reshape(b, n, d)
        return out @ w_out.T + b_out

    def _L1_ffn_ref(input, Wg, W1, b1, W2, b2):
        import jax, jax.numpy as jnp
        import numpy as np
        E = 8
        D = 1024
        H = 256
        TOP_K = 2
        logits = jnp.einsum('bsd,de->bse', input, Wg)
        probs = jax.nn.softmax(logits, axis=-1)
        top_vals, top_idx = jax.lax.top_k(probs, TOP_K)
        top_vals = top_vals / jnp.sum(top_vals, axis=-1, keepdims=True)
        onehot = jax.nn.one_hot(top_idx, E, dtype=input.dtype)
        mask = jnp.sum(onehot, axis=2)
        scores = jnp.sum(onehot * top_vals[..., None], axis=2)
        xm = input[None] * jnp.moveaxis(mask, -1, 0)[..., None]
        h = jnp.einsum('ebsd,edh->ebsh', xm, W1) + b1[:, None, None, :]
        h = jax.nn.relu(h)
        y = jnp.einsum('ebsh,ehd->ebsd', h, W2) + b2[:, None, None, :]
        out = jnp.sum(y * jnp.moveaxis(scores, -1, 0)[..., None], axis=0)
        return out
    edge_index = jnp.stack([src, dst])
    xn = _layernorm(x, axis=-1)
    x = x + _L0_gnn_ref(xn, edge_index, L0_gnn_W, L0_gnn_b) + _L0_mix_ref(xn[None], L0_mix_W_qkv, L0_mix_gamma, L0_mix_beta, L0_mix_W_out, L0_mix_b_out)[0]
    x = x + _L0_ffn_ref(_layernorm(x, axis=-1)[None], L0_ffn_w_gate, L0_ffn_w_up, L0_ffn_w_down)[0]
    xn = _layernorm(x, axis=-1)
    x = x + _L1_gnn_ref(xn, edge_index, edge_type_2, L1_gnn_ln_weight, L1_gnn_W_rel, L1_gnn_W_root, L1_gnn_conv_bias, L1_gnn_wo_weight) + _L1_mix_ref(xn[None], L1_mix_w_qkv, L1_mix_w_out, L1_mix_b_out)[0]
    x = x + _L1_ffn_ref(_layernorm(x, axis=-1)[None], L1_ffn_Wg, L1_ffn_W1, L1_ffn_b1, L1_ffn_W2, L1_ffn_b2)[0]
    return x

_drawn_inputs = setup_inputs


def setup_inputs(seed=0):
    import zlib

    import numpy as np

    out = dict(_drawn_inputs(seed))
    spreads = {'L0_mix_gamma': (1.0, 0.2),
     'L0_mix_beta': (0.0, 0.1),
     'L0_mix_b_out': (0.0, 0.1),
     'L1_gnn_ln_weight': (1.0, 0.6),
     'L1_gnn_conv_bias': (0.0, 2.0),
     'L1_ffn_b1': (0.0, 2.0),
     'L1_ffn_b2': (0.0, 2.0)}
    factors = {'L0_gnn_b': 6.02,
     'L1_gnn_W_rel': 31.379,
     'L1_gnn_W_root': 22.966,
     'L1_gnn_wo_weight': 8.0,
     'L1_mix_w_qkv': 64.0,
     'L1_mix_w_out': 64.0,
     'L1_mix_b_out': 64.0,
     'L1_ffn_Wg': 64.0,
     'L1_ffn_W1': 64.0,
     'L1_ffn_W2': 64.0}
    for name, (base, spread) in spreads.items():
        noise = np.random.default_rng([zlib.crc32(name.encode()), seed]).standard_normal(out[name].shape)
        drawn = base * np.exp(spread * noise) if base else spread * noise
        out[name] = jnp.asarray(drawn.astype(out[name].dtype))
    for name, factor in factors.items():
        out[name] = (out[name] * factor).astype(out[name].dtype)
    return out
```

```python
from contextlib import ExitStack

import numpy as np

import concourse.bass as bass
from concourse import mybir

F32 = mybir.dt.float32
F16 = mybir.dt.float16
I16 = mybir.dt.int16
I32 = mybir.dt.int32
U32 = mybir.dt.uint32
ALU = mybir.AluOpType
ACT = mybir.ActivationFunctionType
AX = mybir.AxisListType

NODES, DIM, EDGES = 1250, 1024, 20000
TN, NT = 125, 10
KD = DIM // 128
HEADS, DH = 16, 64
PAIRS = HEADS // 2
CH = ((0, 500), (500, 500), (1000, 250))
HID = 384
FF, FFP = 286, 288
FB = FFP // 3
NREL = 2
NE, HE = 8, 256
EP, ET = 125, EDGES // 125
ST = 512
NB = NT * NREL
NST = 60
assert NST * ST >= EDGES + NB * (ST - 1) - ST + 1 and NST % 2 == 0

XS, WS, QS, VS, OS0 = 2.0**10, 2.0**8, 2.0**3, 2.0**6, 2.0**6
PS = QS * QS * DH**0.5
OS1, GS, AS, HS, YS = 2.0**4, 2.0**6, 2.0**6, 2.0**4, 2.0**4

SLOTS = [("mix0_qkv", PAIRS), ("mix0_out", 4), ("gnn0", 4), ("ffn_up", 3), ("ffn_down", 1),
         ("gnn1", 3), ("gnn1_out", 1), ("mix1_qkv", PAIRS), ("mix1_out", 4), ("moe", 2 * NE)]
ATT = 16 + 6 * NT
TILES = [("mix0", PAIRS * ATT), ("mix0_out", 4 * NT), ("gnn0", 4 * NT), ("agg0", 2 * NT), ("ffn_up", 18),
         ("ffn_down", 2 * NT), ("gnn1", 5 * NT), ("gnn1_out", 2 * NT), ("mix1", PAIRS * 18),
         ("mix1_out", 4 * NT), ("gate", 30), ("moe", 26 * NE - 6)]
TURNS = [("ln0", NT), ("lnO", NT), ("agg0", 2 * NT), ("ln1", NT), ("ln2", NT), ("gnn1", NT), ("tO", NT), ("ln3", NT)]


def firsts(table):
    at, out = 0, {}
    for name, n in table:
        out[name] = at
        at += n
    return out


SLOT0, TILE0, TURN0 = firsts(SLOTS), firsts(TILES), firsts(TURNS)
Z0 = firsts([(n, NT) for n in ("ln0", "lnO", "agg0", "ln1", "ln2", "tO", "ln3")])
H0 = firsts([(n, NT) for n in ("ln0", "lnO", "ln1", "ln2", "gnn1", "tO", "ln3")])


class Chain:

    def __init__(self, eng, sem):
        self.eng, self.sem, self.base, self.local, self.reg, self.per = eng, sem, 0, 0, None, 0

    def value(self):
        v = self.base + self.local
        return v if self.reg is None else self.reg * self.per + v

    def link(self, ins):
        ins.then_inc(self.sem, 1)
        self.local += 1
        self.eng.wait_ge(self.sem, self.value())

    def add(self, ins):
        ins.then_inc(self.sem, 1)
        self.local += 1

    def enter(self, reg, per):
        self.base, self.local, self.reg, self.per = self.base + self.local, 0, reg, per

    def leave(self, n):
        assert self.local == self.per, (self.local, self.per)
        self.base, self.local, self.reg = self.base + n * self.per, 0, None




def build_program(nc, A, out):

    with ExitStack() as ctx:
        def region(name, size):
            t = ctx.enter_context(nc.sbuf_tensor(name, [128, size // 2], F16))

            def view(off, dt, *shape, parts=128):
                n = int(np.prod(shape)) * (4 if dt in (F32, I32, U32) else 2)
                assert off % 4 == 0 and off + n <= size, (name, off, n, size)
                v = t[0:parts, off // 2:(off + n) // 2]
                if dt != F16:
                    v = v.bitcast(dt)
                names = "abcd"[:len(shape)]
                if len(shape) > 1:
                    v = v.rearrange(f"p ({' '.join(names)}) -> p {' '.join(names)}",
                                    **dict(zip(names[1:], shape[1:])))
                return v
            return view

        def sb(name, shape, dt):
            return ctx.enter_context(nc.sbuf_tensor(name, shape, dt))

        def sem(name):
            return ctx.enter_context(nc.semaphore(name))

        SCR, S1 = 40000, 10000
        R0 = region("R0", SCR + 10032)
        R2 = region("R2", 40960)
        R1 = region("R1", 40960)
        WR = region("WR", 12288 + 4 * 6144)
        SR = region("SR", S1 + 29000)
        XTh, XTl = R0(0, F16, KD, NODES), R0(20000, F16, KD, NODES)
        OT0h, OT0l = R2(0, F16, KD, NODES), R2(20000, F16, KD, NODES)
        X = R1(0, F32, NT, DIM, parts=TN)
        O0 = X
        O1 = R2(0, F32, NT, DIM, parts=TN)
        wst, wsti = WR(0, F32, 3072), WR(0, I32, 3072)
        wh = [WR(12288 + 12288 * s, F16, 3072) for s in range(2)]
        wl = [WR(12288 + 12288 * s + 6144, F16, 3072) for s in range(2)]
        z = [SR(5000 * s, F32, NODES, parts=TN) for s in range(2)]
        bcast = [R0(SCR + 4096 * s, F32, DIM, parts=TN) for s in range(2)]
        xin = [R2(4096 * s, F32, DIM, parts=TN) for s in range(2)]
        scr = [R0(SCR + 2508 * j, F16, NODES) for j in range(4)]
        Kst = [[R2(20120 * s + 2500 * h, F16, NODES) for h in range(2)] for s in range(2)]
        Qst = [[[R2(20120 * s + 5000 + 5000 * h + 2500 * j, F16, NODES) for j in range(2)]
                for h in range(2)] for s in range(2)]
        Vst = [R2(20120 * s + 15000, F16, NT, 2, 128, parts=TN) for s in range(2)]
        Ph = [SR(S1 + 2000 * r, F16, 500, parts=TN) for r in range(4)]
        Pl = [SR(S1 + 2000 * r + 1000, F16, 500, parts=TN) for r in range(4)]
        ot = [SR(S1 + 8000 + 5000 * s, F32, NODES) for s in range(2)]
        ei = SR(S1 + 18000, I32, 3, ET, parts=EP)
        srcf, keyf, blkf, posf = (SR(S1 + 18000 + 1920 + 640 * j, F32, ET, parts=EP) for j in range(4))
        rec = SR(S1 + 22480, F32, ET, 2, parts=EP)
        pos = SR(S1 + 23760, U32, ET, parts=EP)
        minus = SR(S1 + 24400, F32, NST * ST * 2 // 128)
        mask = R1(0, F32, NB, ET, parts=EP)
        zero = R1(12800, F32, NB * ET, parts=EP)
        cum = R1(25600, F32, NB * ET, parts=EP)
        ones, lower = R1(38400, F32, 128), R1(38912, F32, 128)
        small, key_ids = R1(39424, F32, 12, NB, parts=EP), R1(40384, F32, NB, parts=EP)
        smalli = R1(40464, I32, NB, parts=EP)
        st_cmp = R1(0, F32, NST, NB, parts=1)
        Bc = R0(0, I16, NB, NODES, parts=TN)
        es = SR(S1, F32, NST, 4, 2)
        ohd = [SR(S1 + 1920 + 2500 * r, F16, NODES) for r in range(4)]
        ohs = [SR(S1 + 11920 + 252 * r, F16, 126) for r in range(4)]
        iota_n = SR(S1 + 13000, F16, NODES)
        rw = [SR(S1 + 15600 + 2500 * s, F16, NODES, parts=TN) for s in range(2)]
        summed = SR(S1 + 20600, F16, NREL * NODES, parts=TN)
        G0h, G0l = R2(0, F16, NT, DIM, parts=TN), R2(20480, F16, NT, DIM, parts=TN)
        t32 = SR(S1, F32, NT, TN, parts=TN)
        ATh = [SR(S1 + 10000 + 5000 * s, F16, NT, TN, parts=TN) for s in range(2)]
        ATl = [SR(S1 + 12500 + 5000 * s, F16, NT, TN, parts=TN) for s in range(2)]
        HTh, HTl = R2(0, F16, 3, NODES), R2(7500, F16, 3, NODES)
        sg = [R2(15000 + 2000 * s, F32, 500) for s in range(2)]
        hf = [R2(19000 + 2000 * s, F32, 500) for s in range(2)]
        Hh = [SR(S1, F16, NT, FFP, parts=TN), SR(S1 + 11520, F16, NT, FFP, parts=TN)]
        Hl = [SR(S1 + 5760, F16, NT, FFP, parts=TN), R0(SCR, F16, NT, FFP, parts=TN)]
        y = SR(S1 + 17280, F32, NT, FFP, parts=TN)
        Bi = [R2(15000 * s, I16, NT, 250, parts=TN) for s in range(2)]
        Bh = [R2(15000 * s + 5000, F16, NT, 250, parts=TN) for s in range(2)]
        Bl = [R2(15000 * s + 10000, F16, NT, 250, parts=TN) for s in range(2)]
        ye = R2(0, F32, NT, FFP, parts=TN)
        yTh, yTl = R2(12000, F16, 3, NODES), R2(19500, F16, 3, NODES)
        cbias = R2(30000, F32, FF, parts=TN)
        qf = [SR(S1 + 5000 * s, F32, NODES) for s in range(2)]
        kf = [SR(S1 + 10000 + 5120 * s, F32, NT, 128, parts=TN) for s in range(2)]
        vf = [SR(S1 + 20240, F32, NT, 129, parts=TN), R0(SCR, F32, NT, 129, parts=TN)]
        er = [SR(2000 * j, F32, 500) for j in range(4)]
        MHh = [R2(10000 * s, F16, 2, NODES) for s in range(2)]
        MHl = [R2(10000 * s + 5000, F16, 2, NODES) for s in range(2)]
        mr = [R2(20000 + 2000 * s, F32, 500) for s in range(2)]
        b1t = R2(24000, F32, 2, NE)
        b2r = R2(24064, F32, DIM, parts=NE)
        scT = R2(28160, F32, NODES, parts=NE)
        wg_f = R2(33160, F32, KD, NE)
        wg_h, wg_l = R2(33416, F16, KD, NE), R2(33544, F16, KD, NE)
        gs = [R2(33672 + 320 * j, F32, NT, NE, parts=TN) for j in range(8)]
        g1 = [R2(36232 + 40 * j, F32, NT, parts=TN) for j in range(4)]
        gid = R2(36392, F32, NE, parts=TN)

        ident = sb("ident", [128, 128], F32)
        fold = sb("fold", [128, DH], F32)
        stats = sb("stats", [TN, 2, 2, 6], F32)
        mv = sb("mv", [TN, 2, 2], F32)
        rstd = sb("rstd", [TN, 2, 1], F32)
        veps = sb("veps", [TN, 2, 1], F32)
        halves = sb("halves", [TN, NT], F32)
        negm = sb("negm", [TN, 2, 1], F32)
        units = sb("units", [128, 4], F32)
        tick = sb("tick", [TN, 2], F32)
        b1s = sb("b1s", [128, 2, 2], F32)
        nbias = sb("nbias", [TN, 2, 1], F32)
        ssq = sb("ssq", [TN, NT], F32)
        rn = sb("rn", [TN, 2, NT], F32)
        deg = sb("deg", [TN, 3, NT], F32)
        st_ids = sb("st_ids", [1, NST], F32)
        st_off = sb("st_off", [1, NST], F32)
        st_offi = sb("st_offi", [1, NST], I32)
        lnw = sb("lnw", [128, KD], F32)
        dens = sb("dens", [TN, 4], F32)
        kvs = sb("kvs", [128, 2, 130], F32)

        ps = ctx.enter_context(nc.psum_tensor("ps", [128, 4, 512], F32))
        pt = ctx.enter_context(nc.psum_tensor("pt", [128, 2, 2, 512], F32))
        pb = [ps[:, 0:3, :].rearrange("p a b -> p (a b)"),
              pt[:, :, :, :].rearrange("p a b c -> p (a b c)")]

        edges_d = nc.dram_tensor("edges_sorted", (NST * ST, 2), F32, kind="Internal").ap()
        bc_d = nc.dram_tensor("counts", (TN, NB, NODES), I16, kind="Internal").ap()

        const_ready = sem("const_ready")
        w_loaded = sem("w_loaded")
        w_float = sem("w_float")
        w_split = sem("w_split")
        slot_begun = sem("slot_begun")
        mm_done = sem("mm_done")
        evac = sem("evac")
        hi_done = sem("hi_done")
        x_loaded = [sem("x_loaded0"), sem("x_loaded1")]
        mv_ready = sem("mv_ready")
        st_ready = sem("st_ready")
        deg_summed = sem("deg_summed")
        deg_ready, dis_ready, ms_ready, ms_root = sem("deg_ready"), sem("dis_ready"), sem("ms_ready"), sem("ms_root")
        z_normed = sem("z_normed")
        z_ready = sem("z_ready")
        turn_done = sem("turn_done")
        turn_hi = sem("turn_hi")
        turn_lo = sem("turn_lo")
        dve_chain, act_chain, pool_chain = sem("dve_chain"), sem("act_chain"), sem("pool_chain")
        e_loaded = sem("e_loaded")
        e_total = sem("e_total")
        e_sums = sem("e_sums")
        e_pos = sem("e_pos")
        e_clear = sem("e_clear")
        e_moved = sem("e_moved")
        e_back = sem("e_back")
        shuffled = sem("shuffled")
        p_used = sem("p_used")
        acc_out = sem("acc_out")
        fold_done, fold_out = sem("fold_done"), sem("fold_out")
        b_loaded = sem("b_loaded")
        xr_loaded = [sem(f"xr_loaded{i}") for i in range(NT)]
        x_biased = sem("x_biased")
        g_ready = sem("g_ready")
        oh_ready = sem("oh_ready")
        oh_used = sem("oh_used")
        bc_saved = sem("bc_saved")
        t_ready = sem("t_ready")
        at_hi, at_lo = sem("at_hi"), sem("at_lo")
        sg_ready = sem("sg_ready")
        h_hi, h_done = sem("h_hi"), sem("h_done")
        zx_added = sem("zx_added")
        sq_done = sem("sq_done")
        c_loaded = [sem("c_loaded0"), sem("c_loaded1")]
        c_hi, c_lo = sem("c_hi"), sem("c_lo")
        rows_out = sem("rows_out")
        b_free = sem("b_free")
        iota_ready, l_loaded, rn_ready, y_min = sem("iota_ready"), sem("l_loaded"), sem("rn_ready"), sem("y_min")
        y_exp = sem("y_exp")
        y_done = sem("y_done")
        e_min, e_exp, e_relu, k_done = sem("e_min"), sem("e_exp"), sem("e_relu"), sem("k_done")
        kv_done, kv_out, o_done = sem("kv_done"), sem("kv_out"), sem("o_done")
        gate_w, gate_split, g_exp, g_mask, scores_ready = (sem("gate_w"), sem("gate_split"), sem("g_exp"),
                                                           sem("g_mask"), sem("scores_ready"))
        b1_ready = sem("b1_ready")
        m_hi, m_done = sem("m_hi"), sem("m_done")
        stored = sem("stored")

        block = ctx.enter_context(nc.Block())

        def load(eng, n, dst, src):
            if not isinstance(n, int) or n > 0:
                eng.wait_ge(w_split, n)
            eng.dma_start(dst, src).then_inc(w_loaded, 16)

        def one(ap):
            return ap.rearrange("a p n -> p (a n)")

        def turn_view(s, blocks=KD, parts=128, width=TN):
            if blocks <= 4:
                return pt[0:parts, s, 0, 0:blocks * width].rearrange("p (k n) -> p k n", n=width)
            return pt[0:parts, s, :, 0:4 * width].rearrange("p b (k n) -> p b k n", n=width)

        def nodes_of(t, i):
            return t[:, :, bass.ds(i * TN, TN)].rearrange("p (b k) n -> p b k n", b=2)

        def row(t, i):
            return t[:, bass.ds(i, 1)].rearrange("p a n -> p (a n)")

        def piped(make, copy, eng, chain=None, per=0):
            make(0, 0)
            with eng.Fori(0, NT // 2 - 1) as j:
                if chain:
                    chain.enter(j, per)
                for s in range(2):
                    make(j * 2 + (s + 1), 1 - s)
                    copy(j * 2 + s, s)
            if chain:
                chain.leave(NT // 2 - 1)
            make(NT - 1, 1)
            copy(NT - 2, 0)
            copy(NT - 1, 1)

        NORM0 = {"ln0": 0, "lnO": NT, "ln1": 2 * NT, "ln2": 3 * NT, "ln3": 4 * NT}

        def norm_stats(ch, i, s, tile):
            nc.vector.bn_stats(stats[:, s, 0], tile[:, 0:512])
            ch.link(nc.vector.bn_stats(stats[:, s, 1], tile[:, 512:1024]))
            ch.add(nc.vector.tensor_copy(tick[:, 1:2], tick[:, 0:1]))
            nc.vector.bn_aggr(mv[:, s], stats[:, s].rearrange("p a b -> p (a b)")).then_inc(mv_ready, 1)

        def norm_scale(pool, ch, stage, i, s):
            pool.wait_ge(mv_ready, i + (NORM0[stage] + 1))
            ch.add(nc.gpsimd.tensor_tensor(negm[:, s], mv[:, s, 0:1], units[0:TN, 0:1], ALU.mult))
            ch.link(nc.gpsimd.tensor_tensor(veps[:, s], mv[:, s, 1:2], units[0:TN, 1:2], ALU.add))
            ch.link(nc.gpsimd.tensor_tensor(rstd[:, s], veps[:, s], halves[:, 0:1], ALU.pow))
            nc.gpsimd.tensor_tensor(nbias[:, s], negm[:, s], rstd[:, s], ALU.mult).then_inc(st_ready, 1)

        def turn_lows(dve, stage, i, s, hi, lo, scale):
            dve.wait_ge(turn_hi, i + (H0[stage] + 1))
            nc.vector.scalar_tensor_tensor(nodes_of(lo, i), turn_view(s), scale, nodes_of(hi, i),
                                           ALU.mult, ALU.subtract).then_inc(turn_lo, 1)

        def norm_dve(dve, ch, stage, hi, lo, scale, src=X):
            piped(lambda i, s: norm_stats(ch, i, s, row(src, i)),
                  lambda i, s: turn_lows(dve, stage, i, s, hi, lo, scale), dve, ch, 4)

        def norm_act(act, stage, hi, scale, src=X, signal=None):
            r0 = TURN0[stage]

            def make(i, s):
                if stage in NORM0:
                    act.wait_ge(st_ready, i + (NORM0[stage] + 1))
                act.wait_ge(turn_done, i + (r0 - 1))
                if stage == "ln2" and not (isinstance(i, int) and i < 2):
                    act.wait_ge(zx_added, i - 1)
                q = nc.scalar.activation(z[s][:, 0:DIM], row(src, i), ACT.Identity, bias=nbias[:, s],
                                         scale=rstd[:, s]) if stage in NORM0 else \
                    nc.scalar.activation(z[s][:, 0:DIM], row(src, i), ACT.Copy)
                q.then_inc(signal or z_ready, 1)
                if stage == "ln2":
                    act.wait_ge(z_ready, i + (Z0[stage] + 1))
                    nc.scalar.activation(bcast[0], z[s][:, 0:DIM], ACT.Square,
                                         accum_out=ssq[:, bass.ds(i, 1)]).then_inc(sq_done, 1)

            def copy(i, s):
                act.wait_ge(turn_done, i + (r0 + 1))
                nc.scalar.activation(nodes_of(hi, i), turn_view(s), ACT.Copy, scale=scale).then_inc(turn_hi, 1)
            piped(make, copy, act)

        def turn_pe(pe, stage):
            r0 = TURN0[stage]
            with pe.Fori(0, NT // 2) as j:
                for s in range(2):
                    pe.wait_ge(z_ready, j * 2 + (Z0[stage] + s + 1))
                    pe.wait_ge(turn_lo, j * 2 + (r0 + s - 1))
                    turn8(s)

        def turn_ahead(pe, stage, product):
            r0 = TURN0[stage]
            with pe.Fori(0, 3) as j:
                for s in range(2):
                    pe.wait_ge(z_ready, j * 2 + (Z0[stage] + s + 1))
                    pe.wait_ge(turn_lo, j * 2 + (r0 + s - 1))
                    turn8(s)
            for i in range(6, NT):
                pe.wait_ge(z_ready, Z0[stage] + i + 1)
                pe.wait_ge(turn_lo, r0 + i - 1)
                turn8(i % 2)
                product([i - 6])
            pe.wait_ge(turn_lo, r0 + NT)
            product(range(4, NT))

        def turn8(s):
            for k in range(KD):
                t = nc.tensor.transpose(pt[:, s, k // 4, k % 4 * TN:(k % 4 + 1) * TN],
                                        z[s][:, k * 128:(k + 1) * 128], ident[0:TN, 0:TN])
            t.then_inc(turn_done, 1)

        def wait_ring(pe, T):
            if not isinstance(T, int) or T >= 4:
                pe.wait_ge(evac, T - 3)

        def three(o, terms):
            n, first = len(terms), None
            for k, (ah, al, bh, bl) in enumerate(terms):
                m = nc.tensor.matmul(o, ah, bh, start=(k == 0), stop=False)
                first = first or m
                nc.tensor.matmul(o, ah, bl, start=False, stop=False)
                m = nc.tensor.matmul(o, al, bh, start=False, stop=(k == n - 1))
            return first, m

        def gemm_nodes(pe, n, T, b, s, xh, xl, nk, width, chunks, kparts=None, tiles=range(NT)):
            pe.wait_ge(w_split, n + 1)
            kp = kparts or [128] * nk
            Wh, Wl = (w[s][:, 0:nk * width * chunks].rearrange("p (k n) -> p k n", k=nk) for w in (wh, wl))
            for i in tiles:
                for c in range(chunks):
                    t = i * chunks + c
                    wait_ring(pe, T + t)
                    cols, at = slice(c * width, (c + 1) * width), slice(i * TN, (i + 1) * TN)
                    x, m = three(ps[0:TN, (b + t) % 4, 0:width],
                                 [(xh[0:kp[k], k, at], xl[0:kp[k], k, at], Wh[0:kp[k], k, cols], Wl[0:kp[k], k, cols])
                                  for k in range(nk)])
                    if t == 0:
                        x.then_inc(slot_begun, 1)
                    m.then_inc(mm_done, 1)

        def gemm_features(pe, T, b, Wh, Wl, begin=False):
            for c, (off, w) in enumerate(CH):
                wait_ring(pe, T + c)
                x, m = three(ps[:, (b + c) % 4, 0:w],
                             [(Wh(k), Wl(k), XTh[:, k, off:off + w], XTl[:, k, off:off + w]) for k in range(KD)])
                if begin and c == 0:
                    x.then_inc(slot_begun, 1)
                m.then_inc(mm_done, 1)

        def out_loop(eng, stage, tile_stage, body):
            n0, T0 = SLOT0[stage], TILE0[tile_stage]
            with eng.Fori(0, 2) as j:
                for s in range(2):
                    body(j * 2 + (n0 + s), j * (2 * NT) + (T0 + s * NT), (T0 + s * NT) % 4, s, j * 2 + s)

        def add_to_x(dve, T, b, i, cols, scale):
            dve.wait_ge(mm_done, T + 1)
            x = X[:, i, cols]
            nc.vector.scalar_tensor_tensor(x, ps[0:TN, b % 4, 0:x.shape[1]], scale, x,
                                           ALU.mult, ALU.add).then_inc(evac, 1)

        def whole_nodes(T, b, width, chunks, body):
            for i in range(NT):
                for c in range(chunks):
                    body(T + (i * chunks + c), b + i * chunks + c, i, c)

        def qkv0_pe(pe, n, T, s):
            pe.wait_ge(w_split, n + 1)
            W = [w[s].rearrange("p (k j n) -> p k j n", k=KD, j=3) for w in (wh, wl)]
            t = 0
            for j in range(2):
                for off, w in CH:
                    wait_ring(pe, T + t)
                    a, b = three(ps[:, t % 4, 0:w], [(W[0][:, k, j], W[1][:, k, j], XTh[:, k, off:off + w],
                                                          XTl[:, k, off:off + w]) for k in range(KD)])
                    if t == 0:
                        a.then_inc(slot_begun, 1)
                    b.then_inc(mm_done, 1)
                    t += 1
            for i in range(NT):
                wait_ring(pe, T + t)
                a, b = three(ps[0:TN, t % 4, 0:128],
                             [(XTh[:, k, i * TN:(i + 1) * TN], XTl[:, k, i * TN:(i + 1) * TN], W[0][:, k, 2],
                               W[1][:, k, 2]) for k in range(KD)])
                b.then_inc(mm_done, 1)
                t += 1

        def qkv0_act(act, p, T, s):
            for j in range(2):
                for c, (off, w) in enumerate(CH):
                    t = 3 * j + c
                    act.wait_ge(mm_done, T + (t + 1))
                    if t == 0 and not (isinstance(p, int) and p == 0):
                        act.wait_ge(shuffled, p * SHUF)
                    nc.scalar.activation(scr[2 * j][:, off:off + w], ps[:, t % 4, 0:w], ACT.Copy,
                                         scale=QS / (XS * WS)).then_inc(hi_done, 1)
            for i in range(NT):
                t = 6 + i
                act.wait_ge(mm_done, T + (t + 1))
                if i == 0 and not (isinstance(p, int) and p < 2):
                    act.wait_ge(p_used, p * 60 - 60)
                nc.scalar.activation(Vst[s][:, i, :, 0:DH],
                                     ps[0:TN, t % 4, 0:128].rearrange("p (h d) -> p h d", h=2), ACT.Copy,
                                     scale=VS / (XS * WS)).then_inc(hi_done, 1)

        def qkv0_dve(dve, p, T, s):
            for j in range(2):
                for c, (off, w) in enumerate(CH):
                    t = 3 * j + c
                    dve.wait_ge(hi_done, T + (t + 1))
                    q = nc.vector.scalar_tensor_tensor(scr[2 * j + 1][:, off:off + w], ps[:, t % 4, 0:w],
                                                       QS / (XS * WS), scr[2 * j][:, off:off + w],
                                                       ALU.mult, ALU.subtract)
                    q.then_inc(evac, 1)
            for i in range(NT):
                t = 6 + i
                dve.wait_ge(hi_done, T + (t + 1))
                nc.vector.scalar_tensor_tensor(
                    Vst[s][:, i, :, DH:128], ps[0:TN, t % 4, 0:128].rearrange("p (h d) -> p h d", h=2),
                    VS / (XS * WS), Vst[s][:, i, :, 0:DH], ALU.mult, ALU.subtract).then_inc(evac, 1)

        SHUF = 12 * 16

        def shuffle(eng, p, T, s):
            eng.wait_ge(evac, T + 6)
            if not (isinstance(p, int) and p < 2):
                eng.wait_ge(p_used, p * 60 - 60)
            for h in range(2):
                rows = slice(h * DH, (h + 1) * DH)
                for half in range(2):
                    to = slice(half * DH, (half + 1) * DH)
                    eng.dma_start(Kst[s][h][to], scr[2 + half][rows]).then_inc(shuffled, 16)
                    for j in range(2):
                        eng.dma_start(Qst[s][h][j][to], scr[j][rows]).then_inc(shuffled, 16)

        GROUPS = [(h, c) for h in range(2) for c in range(3)]
        SKEW = 2

        def attn_pe(pe, p, T, s):
            units = [(g, kb) for g in range(6) for kb in range(NT)]

            def score(u):
                g, kb = units[u]
                h, c = GROUPS[g]
                off, w = CH[c]
                wait_ring(pe, T + u)
                o = ps[0:TN, u % 4, 0:w]
                nc.tensor.matmul(o, Kst[s][h][:, kb * TN:(kb + 1) * TN], Qst[s][h][0][:, off:off + w],
                                 start=True, stop=False)
                nc.tensor.matmul(o, Kst[s][h][:, kb * TN:(kb + 1) * TN], Qst[s][h][1][:, off:off + w],
                                 start=False, stop=True).then_inc(mm_done, 1)

            pe.wait_ge(shuffled, p * SHUF + SHUF)
            for u in range(SKEW):
                score(u)
            for u in range(60):
                if u + SKEW < 60:
                    score(u + SKEW)
                g, kb = units[u]
                h, c = GROUPS[g]
                off, w = CH[c]
                pe.wait_ge(evac, T + (u + 1))
                if kb == 0 and not (isinstance(p, int) and p == 0 and g < 2):
                    pe.wait_ge(acc_out, p * 6 + (g - 1))
                o = pt[:, 0, g % 2, 0:w]
                nc.tensor.matmul(o, Vst[s][:, kb, h], Ph[u % 4][:, 0:w], start=(kb == 0), stop=False)
                m = nc.tensor.matmul(o, Vst[s][:, kb, h], Pl[u % 4][:, 0:w], start=False, stop=(kb == NT - 1))
                m.then_inc(p_used, 1)
                if kb == NT - 1 and c == 0 and h == 1:
                    fold_pe(pe, p, 0)
            fold_pe(pe, p, 1)

        def fold_pe(pe, p, h):
            pe.wait_ge(acc_out, p * 6 + (3 * h + 3))
            if not (isinstance(p, int) and p == 0 and h == 0):
                pe.wait_ge(fold_out, p * 2 + h)
            for i in range(NT):
                m = nc.tensor.matmul(pt[0:TN, 1, i // 5, i % 5 * DH:(i % 5 + 1) * DH],
                                     ot[h][:, i * TN:(i + 1) * TN], fold[:, :], start=True, stop=True)
            m.then_inc(fold_done, 1)

        def attn_act(act, p, T, s):
            for u in range(60):
                g, kb = divmod(u, NT)
                h, c = GROUPS[g]
                off, w = CH[c]
                act.wait_ge(mm_done, T + (u + 1))
                if not (isinstance(p, int) and p * 60 + u < 4):
                    act.wait_ge(p_used, p * 60 + (u - 3))
                nc.scalar.activation(Ph[u % 4][:, 0:w], ps[0:TN, u % 4, 0:w], ACT.Relu
                                     ).then_inc(hi_done, 1)
                if u % NT == 4 and u >= NT:
                    acc_act(act, p, g - 1)
                if u == 46:
                    fold_act(act, p, 0)
            acc_act(act, p, 5)
            fold_act(act, p, 1)

        def acc_act(act, p, g):
            h, c = GROUPS[g]
            off, w = CH[c]
            act.wait_ge(p_used, p * 60 + (g + 1) * NT)
            if g % 3 == 0 and not (isinstance(p, int) and p == 0):
                act.wait_ge(fold_done, p * 2 + (h - 1))
            nc.scalar.activation(ot[h][:, off:off + w], pt[:, 0, g % 2, 0:w], ACT.Copy,
                                 scale=1.0 / (PS * VS)).then_inc(acc_out, 1)

        def fold_act(act, p, h):
            act.wait_ge(fold_done, p * 2 + (h + 1))
            nc.scalar.activation(
                O0[:, :, bass.ds(p * 128 + h * DH, DH)].rearrange("p (a b) d -> p a b d", a=2),
                pt[0:TN, 1, :, 0:5 * DH].rearrange("p a (b d) -> p a b d", d=DH), ACT.Copy).then_inc(fold_out, 1)

        def attn_dve(dve, p, T, s):
            for u in range(6 * NT):
                w = CH[GROUPS[u // NT][1]][1]
                dve.wait_ge(hi_done, T + (u + 1))
                nc.vector.scalar_tensor_tensor(Pl[u % 4][:, 0:w], ps[0:TN, u % 4, 0:w], 0.0, Ph[u % 4][:, 0:w],
                                               ALU.max, ALU.subtract).then_inc(evac, 1)

        def mix0(eng, qkv, attn):
            T0 = TILE0["mix0"]
            qkv(eng, 0, T0, 0)

            def step(p, s, tail=False):
                if not tail:
                    qkv(eng, p + 1, p * ATT + (T0 + 16), 1 - s)
                    attn(eng, p, p * ATT + (T0 + 32), s)
                else:
                    attn(eng, p, p * ATT + (T0 + 16), s)
            step(0, 0)
            step(1, 1)
            with eng.Fori(1, 3) as j:
                for s in range(2):
                    step(j * 2 + s, s)
            step(6, 0)
            step(7, 1, tail=True)


        def pairs1(eng, first, second, chain=None, per=0):
            T0 = TILE0["mix1"]
            first(0, T0, T0, 0)
            with eng.Fori(0, PAIRS // 2 - 1) as j:
                if chain:
                    chain.enter(j, per)
                for s in range(2):
                    p = j * 2 + s
                    first(j * 2 + (s + 1), j * 36 + (T0 + 13 + 18 * s), T0 + 13 + 18 * s, 1 - s)
                    second(p, j * 36 + (T0 + 26 + 18 * s), T0 + 26 + 18 * s, s)
            if chain:
                chain.leave(PAIRS // 2 - 1)
            p = PAIRS - 2
            first(p + 1, T0 + 13 + 18 * p, T0 + 13 + 18 * p, 1)
            second(p, T0 + 26 + 18 * p, T0 + 26 + 18 * p, 0)
            second(p + 1, T0 + 13 + 18 * (p + 1), T0 + 13 + 18 * (p + 1), 1)

        MT0 = TILE0["gate"] + 1
        MT1 = TILE0["moe"]

        def experts(eng, up, down):
            with eng.Fori(0, NE // 2 - 1) as j:
                for s in range(2):
                    up(eng, j * 2 + (s + 1), j * 52 + (MT1 + 26 * s), 1 - s, MT1 + 26 * s)
                    down(eng, j * 2 + s, j * 52 + (MT1 + 26 * s + 6), s, MT1 + 26 * s + 6)
            e, T = NE - 2, MT1 + 26 * (NE - 2)
            up(eng, e + 1, T, 1, T)
            down(eng, e, T + 6, 0, T + 6)
            down(eng, e + 1, T + 26, 1, T + 26)

        def up_slot(e):
            return SLOT0["moe"] if isinstance(e, int) and e == 0 else e * 2 + (SLOT0["moe"] - 1)

        def moe_up_pe(pe, e, T, s, b=None):
            b = T if b is None else b
            pe.wait_ge(w_split, up_slot(e) + 1)
            par = 0 if isinstance(e, int) and e == 0 else 1
            W = [w[par][:, 0:2048].rearrange("p (k n) -> p k n", k=KD) for w in (wh, wl)]
            for h in range(2):
                cols = slice(h * 128, (h + 1) * 128)
                gemm_features(pe, T + 3 * h, b + 3 * h, lambda k: W[0][:, k, cols], lambda k: W[1][:, k, cols],
                              begin=(h == 0))

        def moe_down_pe(pe, e, T, s, b):
            pe.wait_ge(m_done, e * 6 + 6)
            lastone = isinstance(e, int) and e == NE - 1
            n = e * 2 + (SLOT0["moe"] + 2) if not lastone else SLOT0["moe"] + 2 * NE - 1
            gemm_nodes(pe, n, T, b, 1 if lastone else 0, MHh[s], MHl[s], 2, 512, 2)

        def soft_tiles(soft, p, T, b, s):
            for t in range(13):
                if t < 3:
                    w = CH[t][1]
                    view = lambda a, w=w: a[:, 0:w]
                else:
                    view = lambda a: a[0:TN, 0:128]
                E = p * 13 + t
                soft(T + t, b + t, E, (s + t) % 2, view)

        @block.tensor
        def _(pe):
            pe.wait_ge(const_ready, 1)
            for i in range(NT):
                pe.wait_ge(z_ready, i + 1)
                if i >= 2:
                    pe.wait_ge(turn_lo, i - 1)
                turn8(i % 2)
            pe.wait_ge(e_total, 1)
            pe.wait_ge(turn_lo, NT)
            nc.tensor.matmul(pt[0:EP, 0, 0, 0:NB], lower[0:EP, 0:EP], small[:, 0, :], start=True, stop=True)
            nc.tensor.matmul(pt[0:EP, 0, 1, 0:NB], ones[0:EP, 0:EP], small[:, 0, :], start=True,
                             stop=True).then_inc(e_sums, 1)
            mix0(pe, qkv0_pe, attn_pe)
            pe.wait_ge(fold_out, HEADS)
            T0 = TILE0["mix0_out"]
            turn_ahead(pe, "lnO", lambda tiles: gemm_nodes(pe, 8, T0, T0, 0, OT0h, OT0l, KD, 256, 1, tiles=tiles))
            for i in range(1, 4):
                gemm_nodes(pe, 8 + i, T0 + NT * i, T0 + NT * i, i % 2, OT0h, OT0l, KD, 256, 1)
            out_loop(pe, "gnn0", "gnn0", lambda n, T, b, s, i: gemm_nodes(
                pe, n, T, b, s, XTh, XTl, KD, 256, 1))
            pe.wait_ge(evac, TILE0["agg0"])
            with pe.Fori(0, NST // 2) as j:
                for s in range(2):
                    st = j * 2 + s
                    for q in range(4):
                        pe.wait_ge(oh_ready, st * 4 + (q + 1))
                        if q == 0:
                            pe.wait_ge(rows_out, st + 1)
                        for c, (off, w) in enumerate(((0, 512), (512, 512), (1024, 226))):
                            m = nc.tensor.matmul(pb[s][0:TN, off:off + w], ohs[q][:, 0:TN],
                                                 ohd[q][:, off:off + w], start=(q == 0), stop=(q == 3))
                        m.then_inc(oh_used, 1)
            T0, r0 = TILE0["agg0"], TURN0["agg0"]
            pe.wait_ge(b_free, NST + 2)

            def turn(i, s):
                pe.wait_ge(z_ready, i + (Z0["agg0"] + 1))
                for a in range(2):
                    pe.wait_ge(turn_lo, i * 2 + (r0 + a - 1))
                    for k in range(KD if a == 0 else 2):
                        kk = k + a * KD
                        t = nc.tensor.transpose(pt[0:TN, a, k // 4, k % 4 * TN:(k % 4 + 1) * TN],
                                                z[s][:, kk * TN:(kk + 1) * TN], ident[0:TN, 0:TN])
                    t.then_inc(turn_done, 1)

            def gather(i, s):
                pe.wait_ge(at_lo, i + 1)
                for c in range(2):
                    wait_ring(pe, i * 2 + (T0 + c))
                    _, m = three(ps[0:TN, (T0 + 2 * s + c) % 4, :],
                                 [(ATh[s][:, k], ATl[s][:, k], G0h[:, k, c * 512:(c + 1) * 512],
                                   G0l[:, k, c * 512:(c + 1) * 512]) for k in range(NT)])
                    m.then_inc(mm_done, 1)
            piped(turn, gather, pe)

            def ffn_up(i, c, h):
                n, (off, w) = SLOT0["ffn_up"] + i, CH[c]
                t = TILE0["ffn_up"] + 6 * i + 2 * c + h
                pe.wait_ge(w_split, n + 1)
                V = [half[n % 2][:, 0:2048].rearrange("p (k j n) -> p k j n", k=KD, j=2) for half in (wh, wl)]
                wait_ring(pe, t)
                x, m = three(ps[:, t % 4, 0:w], [(V[0][:, k, h], V[1][:, k, h], XTh[:, k, off:off + w],
                                                  XTl[:, k, off:off + w]) for k in range(KD)])
                if c + h == 0:
                    x.then_inc(slot_begun, 1)
                m.then_inc(mm_done, 1)

            def ffn_ahead(tiles):
                if tiles == [0] or tiles == [2]:
                    ffn_up(0, 0, tiles[0] // 2)
            turn_ahead(pe, "ln1", ffn_ahead)
            for i in range(3):
                for c in range(len(CH)):
                    for h in range(2):
                        if i + c > 0:
                            ffn_up(i, c, h)
            pe.wait_ge(h_done, 9)
            n = SLOT0["ffn_down"]
            gemm_nodes(pe, n, TILE0["ffn_down"], TILE0["ffn_down"], n % 2, HTh, HTl, 3, 512, 2)
            n0, T0 = SLOT0["gnn1"], TILE0["gnn1"]
            turn_ahead(pe, "ln2", lambda tiles: gemm_nodes(pe, n0, T0, T0, n0 % 2, XTh, XTl, KD, FF, 1, tiles=tiles))
            for i in range(1, 3):
                gemm_nodes(pe, n0 + i, T0 + NT * i, T0 + NT * i, (n0 + i) % 2, XTh, XTl, KD, FF, 1)
            pe.wait_ge(h_done, 9 + 2 * NT)
            with pe.Fori(0, NT // 2) as q:
                for r in range(NREL):
                    pe.wait_ge(c_lo, q * 2 + (r + 1))
                    for l in range(2):
                        t = 3 * NT + 2 * r + l
                        wait_ring(pe, q * 4 + (T0 + t))
                        at = slice(l * TN, (l + 1) * TN)
                        _, m = three(ps[0:TN, (T0 + t) % 4, 0:FFP],
                                     [(Bh[r][:, k, at], Bl[r][:, k, at], Hh[r][:, k], Hl[r][:, k])
                                      for k in range(NT)])
                        m.then_inc(mm_done, 1)
            pe.wait_ge(y_done, 1)
            r0 = TURN0["gnn1"]
            for i in range(NT):
                pe.wait_ge(turn_lo, r0 + i - 1)
                for k in range(3):
                    t = nc.tensor.transpose(pt[0:FB, i % 2, 0, k * TN:(k + 1) * TN],
                                            y[:, i, k * FB:(k + 1) * FB], ident[0:TN, 0:TN])
                t.then_inc(turn_done, 1)
            pe.wait_ge(turn_lo, r0 + NT)
            n = SLOT0["gnn1_out"]
            gemm_nodes(pe, n, TILE0["gnn1_out"], TILE0["gnn1_out"], n % 2, yTh, yTl, 3, 512, 2,
                       kparts=[FB, FB, FF - 2 * FB])
            T0 = TILE0["mix1"]

            def qkv1(p, T, b, s):
                pe.wait_ge(w_split, p + (SLOT0["mix1_qkv"] + 1))
                W = [w[s].rearrange("p (k n) -> p k n", k=KD) for w in (wh, wl)]
                gemm_features(pe, T, b, lambda k: W[0][:, k, 0:128], lambda k: W[1][:, k, 0:128], begin=True)
                for i in range(NT):
                    wait_ring(pe, T + (3 + i))
                    at = slice(i * TN, (i + 1) * TN)
                    _, m = three(ps[0:TN, (b + 3 + i) % 4, 0:256],
                                 [(XTh[:, k, at], XTl[:, k, at], W[0][:, k, 128:384], W[1][:, k, 128:384])
                                  for k in range(KD)])
                    m.then_inc(mm_done, 1)

            def attend1(p, T, b, s):
                pe.wait_ge(k_done, p * 13 + 13)
                for i in range(NT):
                    m = nc.tensor.matmul(pt[:, 0, s, 0:129], kf[s][:, i], vf[s][:, i], start=(i == 0),
                                         stop=(i == NT - 1))
                m.then_inc(kv_done, 1)
                pe.wait_ge(kv_out, p + 1)
                for a in range(5):
                    wait_ring(pe, T + a)
                    for l in range(2):
                        i = 2 * a + l
                        m = nc.tensor.matmul(ps[0:TN, (b + a) % 4, l * 130:(l + 1) * 130],
                                             qf[s][:, i * TN:(i + 1) * TN], kvs[:, s], start=True, stop=True)
                    m.then_inc(mm_done, 1)
            pairs1(pe, qkv1, attend1)
            T0 = TILE0["mix1_out"]
            turn_ahead(pe, "tO", lambda tiles: gemm_nodes(pe, 32, T0, T0, 0, XTh, XTl, KD, 256, 1, tiles=tiles))
            for i in range(1, 4):
                gemm_nodes(pe, 32 + i, T0 + NT * i, T0 + NT * i, i % 2, XTh, XTl, KD, 256, 1)
            turn_pe(pe, "ln3")
            pe.wait_ge(turn_lo, TURN0["ln3"] + NT)
            T = TILE0["gate"]
            pe.wait_ge(gate_split, 1)
            wait_ring(pe, T)
            for i in range(NT):
                at = slice(i * TN, (i + 1) * TN)
                _, m = three(ps[0:TN, T % 4, i * NE:(i + 1) * NE],
                             [(XTh[:, k, at], XTl[:, k, at], wg_h[:, k], wg_l[:, k]) for k in range(KD)])
            m.then_inc(mm_done, 1)
            moe_up_pe(pe, 0, MT0, 0)
            pe.wait_ge(scores_ready, 1)
            for a in range(3):
                t = TILE0["gate"] + 7 + a
                wait_ring(pe, t)
                for l in range(4 if a < 2 else 2):
                    m = nc.tensor.matmul(ps[0:NE, t % 4, l * TN:(l + 1) * TN], gs[5][:, 4 * a + l],
                                         ident[0:TN, 0:TN], start=True, stop=True)
                m.then_inc(mm_done, 1)
            pe.wait_ge(evac, TILE0["gate"] + 10)
            for i in range(NT):
                for c in range(2):
                    t = TILE0["gate"] + 10 + 2 * i + c
                    wait_ring(pe, t)
                    nc.tensor.matmul(ps[0:TN, t % 4, :], scT[:, i * TN:(i + 1) * TN],
                                     b2r[:, c * 512:(c + 1) * 512], start=True, stop=True).then_inc(mm_done, 1)
            experts(pe, moe_up_pe, moe_down_pe)

        @block.scalar
        def _(act):
            for i in range(-1, NT):
                if i + 1 < NT:
                    s = (i + 1) % 2
                    act.wait_ge(st_ready, i + 2)
                    if i + 1 >= 2:
                        act.wait_ge(turn_done, i)
                    nc.scalar.activation(z[s][:, 0:DIM], xin[s], ACT.Identity, bias=nbias[:, s],
                                         scale=rstd[:, s]).then_inc(z_ready, 1)
                if i >= 0:
                    act.wait_ge(turn_done, i + 1)
                    nc.scalar.activation(nodes_of(XTh, i), turn_view(i % 2), ACT.Copy, scale=XS).then_inc(turn_hi, 1)
            mix0(act, qkv0_act, attn_act)
            norm_act(act, "lnO", OT0h, OS0, signal=z_normed)
            with act.Fori(0, NST // 2) as j:
                for s in range(2):
                    st = j * 2 + s
                    act.wait_ge(oh_used, st * 4 + 4)
                    act.wait_ge(b_free, st + 1)
                    nc.scalar.activation(rw[s], pb[s][0:TN, 0:NODES], ACT.Copy).then_inc(rows_out, 1)
            act.wait_ge(b_free, NST + 2)
            for i in range(NT // 2, NT):
                if i > NT // 2:
                    act.wait_ge(deg_summed, i - NT // 2)
                nc.scalar.activation(summed, Bc[:, NREL * i:NREL * (i + 1)].rearrange("p r n -> p (r n)"), ACT.Copy,
                                     accum_out=deg[:, 0, i:i + 1]).then_inc(deg_summed, 1)
            T0, r0 = TILE0["agg0"], TURN0["agg0"]
            with act.Fori(0, NT // 2) as j:
                for s in range(2):
                    i = j * 2 + s
                    act.wait_ge(t_ready, i + 1)
                    act.wait_ge(mm_done, i * 2 + (T0 - 2))
                    nc.scalar.activation(ATh[s], t32, ACT.Copy).then_inc(at_hi, 1)
            act.wait_ge(bc_saved, 16)
            norm_act(act, "ln1", XTh, XS)
            for u in range(9):
                T = TILE0["ffn_up"] + 2 * u
                w = CH[u % 3][1]
                act.wait_ge(mm_done, T + 1)
                if u >= 2:
                    act.wait_ge(h_done, u - 1)
                nc.scalar.activation(sg[u % 2][:, 0:w], ps[:, T % 4, 0:w], ACT.Silu,
                                     scale=1.0 / (127.0 * XS)).then_inc(sg_ready, 1)
            norm_act(act, "ln2", XTh, XS)
            T0 = TILE0["gnn1"] + NT
            for r in range(NREL):
                for i in range(NT):
                    T = T0 + r * NT + i
                    act.wait_ge(mm_done, T + 1)
                    act.wait_ge(h_done, 9)
                    if r + i == 0:
                        act.wait_ge(rn_ready, 1)
                    nc.scalar.activation(Hh[r][:, i, 0:FF], ps[0:TN, T % 4, 0:FF], ACT.Copy,
                                         scale=rn[:, 1, i:i + 1]).then_inc(h_hi, 1)
            with act.Fori(0, NT // 2) as q:
                for r in range(NREL):
                    act.wait_ge(c_loaded[r], q * 16 + 16)
                    act.wait_ge(mm_done, q * 4 + (TILE0["gnn1"] + 3 * NT + 2 * r - 2))
                    nc.scalar.activation(Bh[r], Bi[r], ACT.Copy).then_inc(c_hi, 1)
            act.wait_ge(y_min, 1)
            nc.scalar.activation(ye, ye, ACT.Exp).then_inc(y_exp, 1)
            r0 = TURN0["gnn1"]
            for i in range(NT):
                act.wait_ge(turn_done, r0 + i + 1)
                nc.scalar.activation(yTh[0:FB, :, i * TN:(i + 1) * TN], turn_view(i % 2, 3, FB), ACT.Copy,
                                     scale=YS).then_inc(turn_hi, 1)
            def soft(T, b, E, s, view):
                e = s
                act.wait_ge(mm_done, T + 1)
                if not isinstance(E, int) or E >= 2:
                    act.wait_ge(k_done, E - 1)
                nc.scalar.activation(view(er[e]), view(ps[:, b % 4, :]), ACT.Relu,
                                     scale=1.0 / (XS * WS)).then_inc(e_relu, 1)
                act.wait_ge(evac, T + 1)
                nc.scalar.activation(view(er[2 + e]), view(er[2 + e]), ACT.Exp).then_inc(e_exp, 1)

            pairs1(act, lambda p, T, b, s: soft_tiles(soft, p, T, b, s), lambda p, T, b, s: None)
            act.wait_ge(evac, TILE0["mix1_out"])
            norm_act(act, "tO", XTh, OS1, src=O1)
            norm_act(act, "ln3", XTh, XS)
            def up(eng, e, T, s, b=None):
                b = T if b is None else b
                nc.scalar.activation(b1s[:, s], (b1t[:, :, bass.ds(e, 1)] if not isinstance(e, int)
                                                 else b1t[:, :, e:e + 1]).rearrange("p h a -> p (h a)"),
                                     ACT.Copy).then_inc(b1_ready, 1)
                act.wait_ge(b1_ready, e + 1)
                for h in range(2):
                    for c, (off, w) in enumerate(CH):
                        t = 3 * h + c
                        act.wait_ge(mm_done, T + (t + 1))
                        nc.scalar.activation(MHh[s][:, h, off:off + w], ps[:, (b + t) % 4, 0:w], ACT.Relu,
                                             bias=b1s[:, s, h:h + 1],
                                             scale=1.0 / (XS * WS)).then_inc(m_hi, 1)
            act.wait_ge(g_mask, 1)
            nc.scalar.activation(gs[2], gs[1], ACT.Exp).then_inc(g_exp, 1)
            act.wait_ge(gate_w, 64)
            up(act, 0, MT0, 0)
            experts(act, up, lambda *a: None)

        @block.gpsimd
        def _(pool):
            g = nc.gpsimd
            ch = Chain(pool, pool_chain)
            for t, v in ((ident[:, :], 0.0), (fold[:, :], 0.0), (lower, 1.0), (minus, -1.0)):
                ch.link(g.memset(t, v))
            g.memset(ones, 1.0)
            ch.link(g.affine_select(out=ident[:, :], in_=ident[:, :], compare_op=ALU.not_equal, fill=1.0,
                                    base=0, pattern=[[-1, 128]], channel_multiplier=1))
            for b in (0, -DH):
                ch.link(g.affine_select(out=fold[:, :], in_=fold[:, :], compare_op=ALU.not_equal, fill=1.0,
                                        base=b, pattern=[[-1, DH]], channel_multiplier=1))
            ch.link(g.affine_select(out=lower, in_=lower, compare_op=ALU.is_gt, fill=0.0,
                                    base=0, pattern=[[1, 128]], channel_multiplier=-1))
            g.iota(key_ids, pattern=[[1, NB]], base=0, channel_multiplier=0, allow_small_or_imprecise_dtypes=True)
            ch.link(g.iota(st_ids[:, :], pattern=[[1, NST]], base=0, channel_multiplier=0,
                           allow_small_or_imprecise_dtypes=True))
            ch.link(g.memset(kvs[:, :, :], 0.0))
            ch.link(g.memset(halves[:, :], -0.5))
            for c, u in enumerate((-1.0, 1e-5, WS, 1.0)):
                ch.link(g.memset(units[:, c:c + 1], u))
            g.memset(st_off[:, :], 0.0).then_inc(const_ready, 1)
            pool.wait_ge(const_ready, 1)
            pool.dma_start(edges_d.rearrange("(p s) c -> p (s c)", p=128), minus).then_inc(e_clear, 16)

            def split(n, s, width, parts=128, scale=WS):
                if not isinstance(n, int) or n >= 2:
                    pool.wait_ge(slot_begun, n)
                if scale == 1.0:
                    pool.wait_ge(w_float, n - SLOT0["ffn_up"] + 1)
                else:
                    pool.wait_ge(w_loaded, 16 * n + 16)
                if width == KD * FF:
                    v = wst[:, 0:width].rearrange("p (k n) -> p k n", k=KD)
                    ch.link(g.tensor_tensor(v, v, lnw[:, :].unsqueeze(2).to_broadcast([128, KD, FF]), ALU.mult))
                w, hi = wst[0:parts, 0:width], wh[s][0:parts, 0:width]
                if scale != 1.0:
                    ch.link(g.tensor_tensor(w, w, units[0:parts, 2:3].to_broadcast([parts, width]), ALU.mult))
                ch.link(g.tensor_tensor(hi, w, units[0:parts, 3:4].to_broadcast([parts, width]), ALU.mult))
                g.tensor_tensor(wl[s][0:parts, 0:width], w, hi, ALU.subtract).then_inc(w_split, 1)

            def split_loop(n0, count, width):
                with pool.Fori(0, count // 2) as j:
                    ch.enter(j, 4)
                    for s in range(2):
                        split(j * 2 + (n0 + s), (n0 + s) % 2, width)
                ch.leave(count // 2)

            def norm_pool(stage):
                with pool.Fori(0, NT // 2) as j:
                    ch.enter(j, 6)
                    for s in range(2):
                        norm_scale(pool, ch, stage, j * 2 + s, s)
                ch.leave(NT // 2)

            def add_bias(n, bias):
                pool.wait_ge(b_loaded, 16 * n)
                for i in range(NT):
                    if n == 3:
                        pool.wait_ge(xr_loaded[i], 16)
                    g.tensor_tensor(X[:, i], X[:, i], bias, ALU.add).then_inc(x_biased, 1)

            for i in range(NT):
                norm_scale(pool, ch, "ln0", i, i % 2)
            split(0, 0, 3072)
            split(1, 1, 3072)
            pool.wait_ge(e_pos, 1)
            pool.wait_ge(e_clear, 16)
            for n in range(2, 8):
                split(n, n % 2, 3072)
                for t in range((n - 2) * ET // 6, (n - 1) * ET // 6):
                    g.indirect_dma_start(edges_d, bass.IndirectOffsetOnAxis(pos[:, t:t + 1], 0),
                                         rec[:, t, :], None).then_inc(e_moved, 16)
            split(8, 0, 2048)
            pool.wait_ge(b_loaded, 32)

            def affine(i, s):
                v = z[s][:, 0:DIM]
                pool.wait_ge(z_normed, i + 1)
                ch.link(g.tensor_tensor(v, v, bcast[0], ALU.mult))
                g.tensor_tensor(v, v, bcast[1], ALU.add).then_inc(z_ready, 1)
            piped(lambda i, s: norm_scale(pool, ch, "lnO", i, s), affine, pool, ch, 8)
            add_bias(3, bcast[0])
            for n in (9, 10, 11):
                split(n, n % 2, 2048)
            split_loop(12, 4, 2048)
            g.iota(iota_n, pattern=[[1, NODES]], base=0, channel_multiplier=0,
                   allow_small_or_imprecise_dtypes=True).then_inc(iota_ready, 1)
            pool.wait_ge(deg_ready, 1)
            pool.wait_ge(deg_summed, NT - NT // 2)
            ch.link(g.tensor_scalar(deg[:, 0], deg[:, 0], 1.0, None, ALU.add))
            g.tensor_tensor(deg[:, 0], deg[:, 0], halves[:, :], ALU.pow).then_inc(dis_ready, 1)
            with pool.Fori(0, NT // 2) as j:
                for s in range(2):
                    pool.wait_ge(at_hi, j * 2 + (s + 1))
                    g.tensor_tensor(ATl[s], t32, ATh[s], ALU.subtract).then_inc(at_lo, 1)
            split(16, 0, 2048, scale=1.0)
            norm_pool("ln1")
            for n in range(17, 20):
                split(n, n % 2, 2048 if n < 19 else 3072, scale=1.0)
            pool.wait_ge(l_loaded, 32)
            split(20, 0, KD * FF)

            def residual(i, s):
                pool.wait_ge(z_ready, i + (Z0["ln2"] + 1))
                x = row(X, i)
                g.tensor_tensor(x, x, z[s][:, 0:DIM], ALU.add).then_inc(zx_added, 1)
            piped(lambda i, s: norm_scale(pool, ch, "ln2", i, s), residual, pool, ch, 6)
            pool.wait_ge(ms_ready, 1)
            g.tensor_tensor(ssq[:, :], ssq[:, :], halves[:, :], ALU.pow).then_inc(ms_root, 1)
            split(21, 1, KD * FF)
            split(22, 0, KD * FF)
            split(23, 1, 3072, FB)
            split_loop(24, 8, 3072)
            split(32, 0, 2048)
            add_bias(5, bcast[1])
            for n in (33, 34, 35):
                split(n, n % 2, 2048)
            norm_pool("ln3")
            split_loop(36, 16, 2048)

        @block.sync
        def _(sp):
            for j, n in enumerate(("src", "dst", "edge_type_2")):
                sp.dma_start(ei[:, j], A[n].rearrange("(p t) -> p t", p=EP)).then_inc(e_loaded, 16)
            sp.dma_start(lnw[:, :], A["ln_weight"]).then_inc(l_loaded, 16)
            x_t = A["x"].rearrange("(t p) c -> t p c", p=TN)
            for i in range(NT):
                if i >= 2:
                    sp.wait_ge(z_ready, i - 1)
                sp.dma_start(xin[i % 2], x_t[i]).then_inc(x_loaded[i % 2], 16)
                if i == 1:
                    load(sp, 0, wst, A["w_mix0"][0])
            load(sp, 1, wst, A["w_mix0"][1])
            load(sp, 2, wst, A["w_mix0"][2])
            shuffle(sp, 0, 0, 0)
            load(sp, 3, wst, A["w_mix0"][3])
            shuffle(sp, 1, 16, 1)
            with sp.Fori(1, 3) as j:
                for s in range(2):
                    p = j * 2 + s
                    load(sp, p + 2, wst, one(A["w_mix0"][bass.ds(p + 2, 1)]))
                    shuffle(sp, p, p * ATT + (16 - ATT), s)
            load(sp, 8, wst[:, 0:2048], A["w_out0"][0])
            shuffle(sp, 6, 16 + 5 * ATT, 0)
            shuffle(sp, 7, 16 + 6 * ATT, 1)
            sp.wait_ge(shuffled, SHUF * PAIRS)
            for j, n in enumerate(("L0_mix_gamma", "L0_mix_beta")):
                sp.dma_start(bcast[j], A[n].unsqueeze(0).to_broadcast([TN, DIM])).then_inc(b_loaded, 16)
            for i in range(NT):
                sp.wait_ge(turn_done, TURN0["lnO"] + i + 1)
                sp.dma_start(X[:, i], x_t[i]).then_inc(xr_loaded[i], 16)
            sp.wait_ge(z_ready, Z0["lnO"] + NT)
            for j, n in enumerate(("L0_mix_b_out", "L0_gnn_b")):
                sp.dma_start(bcast[j], A[n].unsqueeze(0).to_broadcast([TN, DIM])).then_inc(b_loaded, 16)
                sp.wait_ge(b_loaded, 16 * (3 + j))
            for n in (9, 10, 11):
                load(sp, n, wst[:, 0:2048], A["w_out0"][n - 8])
            with sp.Fori(0, 4) as i:
                load(sp, i + 12, wst[:, 0:2048], one(A["w_gnn0"][bass.ds(i, 1)]))
            sp.wait_ge(e_moved, 16 * ET)
            sp.wait_ge(fold_out, HEADS)
            sp.dma_start(es, edges_d.rearrange("(t p q) c -> p t q c", p=128, q=4)).then_inc(e_back, 16)
            load(sp, 16, wsti[:, 0:2048], A["w_up0"][0])
            sp.wait_ge(b_free, NST + 2)
            sp.dma_start(bc_d, Bc).then_inc(bc_saved, 16)
            for n in (17, 18):
                load(sp, n, wsti[:, 0:2048], A["w_up0"][n - 16])
            load(sp, 19, wsti, A["w_down0"][0])
            load(sp, 20, wst[:, 0:KD * FF], A["w_gnn1"][0])
            sp.wait_ge(mm_done, TILE0["gnn1"])
            sp.dma_start(cbias, A["L1_gnn_conv_bias"].unsqueeze(0).to_broadcast([TN, FF])).then_inc(l_loaded, 16)
            for n in (21, 22):
                load(sp, n, wst[:, 0:KD * FF], A["w_gnn1"][n - 20])
            sp.wait_ge(w_split, 23)
            sp.dma_start(wst[0:FB, :], A["w_gnn1_out"]).then_inc(w_loaded, 16)
            bv = bc_d.rearrange("p (b r) (q c) -> r q p b c", r=NREL, q=5)
            for r in range(NREL):
                sp.dma_start(Bi[r], bv[r, 0]).then_inc(c_loaded[r], 16)
            with sp.Fori(1, 5) as q:
                for r in range(NREL):
                    sp.wait_ge(c_lo, q * 2 + (r - 1))
                    sp.dma_start(Bi[r], bv[r, bass.ds(q, 1)].rearrange("q p b c -> p (q b) c")
                                 ).then_inc(c_loaded[r], 16)
            with sp.Fori(0, PAIRS) as i:
                load(sp, i + 24, wst, one(A["w_mix1"][bass.ds(i, 1)]))
            load(sp, 32, wst[:, 0:2048], A["w_out1"][0])
            sp.wait_ge(evac, TILE0["mix1_out"])
            sp.dma_start(bcast[1], A["L1_mix_b_out"].unsqueeze(0).to_broadcast([TN, DIM])).then_inc(b_loaded, 16)
            for n in (33, 34, 35):
                load(sp, n, wst[:, 0:2048], A["w_out1"][n - 32])
            sp.wait_ge(turn_done, TURN0["tO"] + NT)
            sp.dma_start(b1t, A["b1"]).then_inc(gate_w, 16)
            sp.dma_start(b2r, A["L1_ffn_b2"]).then_inc(gate_w, 16)
            sp.dma_start(wg_f, A["L1_ffn_Wg"].rearrange("(k p) e -> p k e", p=128)).then_inc(gate_w, 16)
            sp.dma_start(gid, A["rev"].unsqueeze(0).to_broadcast([TN, NE])).then_inc(gate_w, 16)
            with sp.Fori(0, 2 * NE) as i:
                load(sp, i + 36, wst[:, 0:2048], one(A["w_moe"][bass.ds(i, 1)]))
            out_t = out.rearrange("(t p) c -> t p c", p=TN)
            for i in range(NT):
                sp.wait_ge(evac, MT1 + 26 * (NE - 1) + 2 * i + 2)
                sp.dma_start(out_t[i], X[:, i]).then_inc(stored, 16)
            sp.wait_ge(stored, 16 * NT)

        @block.vector
        def _(dve):
            v = nc.vector
            ch = Chain(dve, dve_chain)

            def stt(o, a, scalar, b, op0, op1):
                return v.scalar_tensor_tensor(o, a, scalar, b, op0, op1)

            ch.link(v.memset(tick[:, :], 0.0))
            for i in range(-1, NT):
                if i + 1 < NT:
                    s = (i + 1) % 2
                    dve.wait_ge(x_loaded[s], 16 * ((i + 1) // 2 + 1))
                    norm_stats(ch, i + 1, s, xin[s])
                if i >= 0:
                    turn_lows(dve, "ln0", i, i % 2, XTh, XTl, XS)

            dve.wait_ge(e_loaded, 48)
            dve.wait_ge(const_ready, 1)
            ch.link(v.tensor_copy(srcf, ei[:, 0]))
            ch.link(v.tensor_copy(rec[:, :, 1], ei[:, 1]))
            ch.link(v.tensor_copy(keyf, ei[:, 2]))
            ch.link(v.tensor_scalar(blkf, srcf, float(TN), None, ALU.is_ge))
            for b in range(2, NT):
                ch.link(stt(blkf, srcf, float(TN * b), blkf, ALU.is_ge, ALU.add))
            ch.link(stt(keyf, blkf, float(NREL), keyf, ALU.mult, ALU.add))
            ch.link(stt(rec[:, :, 0], blkf, -float(TN), srcf, ALU.mult, ALU.add))
            ch.link(v.memset(zero, 0.0))
            ch.link(v.tensor_tensor(mask, keyf.unsqueeze(1).to_broadcast([EP, NB, ET]),
                                    key_ids.unsqueeze(2).to_broadcast([EP, NB, ET]), ALU.is_equal))
            ch.link(v.tensor_tensor_scan(cum, mask.rearrange("p b t -> p (b t)"), zero, 0.0, ALU.add, ALU.add))
            cum3 = cum.rearrange("p (b t) -> p b t", t=ET)
            ends = cum3[:, :, ET - 1]
            ch.link(v.tensor_copy(small[:, 1], ends))
            ch.link(v.tensor_copy(small[:, 0, 0:1], small[:, 1, 0:1]))
            v.tensor_tensor(small[:, 0, 1:NB], small[:, 1, 1:NB], small[:, 1, 0:NB - 1],
                            ALU.subtract).then_inc(e_total, 1)
            dve.wait_ge(e_sums, 1)
            ch.link(v.tensor_scalar(smalli, pt[0:EP, 0, 1, 0:NB], float(ST - 1), None, ALU.add))
            ch.link(v.tensor_scalar(smalli, smalli, ST.bit_length() - 1, None, ALU.logical_shift_right))
            ch.link(v.tensor_copy(small[:, 2], smalli))
            ch.link(v.tensor_tensor_scan(small[:, 3], small[:, 2], zero[:, 0:NB], 0.0, ALU.add, ALU.add))
            ch.link(v.tensor_tensor(small[:, 4], small[:, 3], small[:, 2], ALU.subtract))
            ch.link(stt(small[:, 5], small[:, 4], float(ST), pt[0:EP, 0, 0, 0:NB], ALU.mult, ALU.add))
            ch.link(v.tensor_tensor(small[:, 6], small[:, 5], small[:, 1], ALU.subtract))
            ch.link(v.tensor_tensor(small[:, 7], small[:, 6], small[:, 0], ALU.add))
            ch.link(v.tensor_scalar(small[:, 8], small[:, 7], -1.0, None, ALU.add))
            ch.link(v.tensor_tensor(cum3, cum3, small[:, 8].unsqueeze(2).to_broadcast([EP, NB, ET]), ALU.add))
            ch.link(v.tensor_tensor(cum3, cum3, mask, ALU.mult))
            ch.link(v.tensor_reduce(posf, cum3.rearrange("p b t -> p t b"), AX.X, ALU.add))
            v.tensor_copy(pos, posf).then_inc(e_pos, 1)
            dve.wait_ge(e_pos, 1)
            ch.link(v.tensor_tensor(st_cmp, st_ids[:, :].unsqueeze(2).to_broadcast([1, NST, NB]),
                                    small[0:1, 3].unsqueeze(1).to_broadcast([1, NST, NB]), ALU.is_ge))
            ch.link(v.tensor_reduce(st_off[:, :], st_cmp, AX.X, ALU.add))
            ch.link(v.tensor_scalar(st_off[:, :], st_off[:, :], float(NB - 1), float(NODES), ALU.min, ALU.mult))
            ch.link(v.tensor_copy(st_offi[:, :], st_off[:, :]))
            mix0(dve, qkv0_dve, attn_dve)
            dve.wait_ge(fold_out, HEADS)
            norm_dve(dve, ch, "lnO", OT0h, OT0l, OS0, src=O0)
            for i in range(4):
                for k in range(NT):
                    if i == 0:
                        dve.wait_ge(x_biased, k + 1)
                    T = TILE0["mix0_out"] + NT * i + k
                    add_to_x(dve, T, T, k, slice(i * 256, (i + 1) * 256), 1.0 / (OS0 * WS))
            dve.wait_ge(b_loaded, 64)
            tmp = [z[s][:, 0:256] for s in range(2)]

            def put_g(T, b, i, cols, u):
                dve.wait_ge(mm_done, T + 1)
                stt(tmp[u], ps[0:TN, b % 4, 0:256], 1.0 / (XS * WS), bcast[1][:, cols],
                    ALU.mult, ALU.add).then_inc(evac, 1)
                dve.wait_ge(evac, T + 1)
                ch.link(v.tensor_scalar(G0h[:, i, cols], tmp[u], GS, None, ALU.mult))
                stt(G0l[:, i, cols], tmp[u], GS, G0h[:, i, cols], ALU.mult, ALU.subtract).then_inc(g_ready, 1)
            n0, T0 = SLOT0["gnn0"], TILE0["gnn0"]
            with dve.Fori(0, 2) as j:
                ch.enter(j, 2 * NT)
                for s in range(2):
                    for i in range(NT):
                        put_g(j * (2 * NT) + (T0 + s * NT + i), T0 + s * NT + i, i,
                              bass.ds(j * 512 + s * 256, 256), i % 2)
            ch.leave(2)
            dve.wait_ge(g_ready, 4 * NT)
            ch.link(v.memset(Bc.rearrange("p a b -> p (a b)").bitcast(F32), 0.0))
            v.engine_nop().then_inc(b_free, 2)
            v.engine_nop().then_inc(rows_out, 2)
            dve.wait_ge(e_back, 16)
            dve.wait_ge(iota_ready, 1)
            flat = Bc.rearrange("p a b -> p (a b)")

            def hot(st, q, first=False):
                if not first:
                    dve.wait_ge(oh_used, st * 4 + (q - 3))
                e = es[:, bass.ds(st, 1), q].rearrange("p a c -> p (a c)")
                v.tensor_scalar(ohd[q], iota_n, e[:, 1:2], None, ALU.is_equal)
                v.tensor_scalar(ohs[q], iota_n[:, 0:126], e[:, 0:1], None, ALU.is_equal).then_inc(oh_ready, 1)

            def add_rows(st, s):
                off = dve.value_load(st_offi[0:1, bass.ds(st, 1)], min_val=0, max_val=(NB - 1) * NODES)
                dve.wait_ge(rows_out, st + 3)
                dve.wait_ge(b_free, st + 2)
                rows = flat[:, bass.ds(off, NODES)]
                v.tensor_tensor(rows, rows, rw[s], ALU.add).then_inc(b_free, 1)

            for q in range(4):
                hot(0, q, first=True)
            with dve.Fori(0, NST // 2 - 1) as j:
                for s in range(2):
                    for q in range(4):
                        hot(j * 2 + (s + 1), q)
                    add_rows(j * 2 + s, s)
            for q in range(4):
                hot(NST - 1, q)
            add_rows(NST - 2, 0)
            add_rows(NST - 1, 1)
            dve.wait_ge(b_free, NST + 2)
            ch.link(v.tensor_reduce(deg[:, 0, 0:NT // 2], Bc.rearrange("p (i r) n -> p i (r n)", r=NREL)[:, 0:NT // 2],
                                    AX.X, ALU.add))
            v.engine_nop().then_inc(deg_ready, 1)
            dve.wait_ge(dis_ready, 1)
            ch.link(v.tensor_scalar(deg[:, 1], deg[:, 0], AS, None, ALU.mult))
            ch.link(v.tensor_scalar(deg[:, 2], deg[:, 0], 1.0 / (AS * GS), None, ALU.mult))
            T0, r0 = TILE0["agg0"], TURN0["agg0"]

            def make(i, s):
                dve.wait_ge(turn_done, i * 2 + (r0 - 2))
                v.tensor_tensor(z[s], row(Bc, i * 2), row(Bc, i * 2 + 1), ALU.add).then_inc(z_ready, 1)
                dve.wait_ge(turn_done, i * 2 + (r0 + 1))
                if not (isinstance(i, int) and i == 0):
                    dve.wait_ge(at_lo, i)
                v.tensor_tensor(t32[:, 0:KD].rearrange("p (b k) n -> p b k n", b=2), turn_view(0, parts=TN),
                                deg[:, 1, 0:KD].rearrange("p (b k) -> p b k", b=2).unsqueeze(3)
                                .to_broadcast([TN, 2, 4, TN]), ALU.mult).then_inc(turn_lo, 1)
                dve.wait_ge(turn_done, i * 2 + (r0 + 2))
                v.tensor_tensor(t32[:, KD:NT], turn_view(1, 2, parts=TN),
                                deg[:, 1, KD:NT].unsqueeze(2).to_broadcast([TN, 2, TN]),
                                ALU.mult).then_inc(turn_lo, 1)
                dve.wait_ge(turn_lo, i * 2 + (r0 + 2))
                d = row(t32, i)
                stt(d, ident[0:TN, 0:TN], deg[:, 1, bass.ds(i, 1)], d, ALU.mult, ALU.add).then_inc(t_ready, 1)

            def put(i, s):
                for c in range(2):
                    T, x = i * 2 + (T0 + c), row(X, i)[:, c * 512:(c + 1) * 512]
                    dve.wait_ge(mm_done, T + 1)
                    stt(x, ps[0:TN, (T0 + 2 * s + c) % 4, :], deg[:, 2, bass.ds(i, 1)], x,
                        ALU.mult, ALU.add).then_inc(evac, 1)
            piped(make, put, dve)
            dve.wait_ge(evac, TILE0["ffn_up"])
            dve.wait_ge(bc_saved, 16)

            def to_float(n, width):
                dve.wait_ge(w_loaded, 16 * (n + 1))
                v.tensor_copy(wst[:, 0:width], wsti[:, 0:width]).then_inc(w_float, 1)
            to_float(16, 2048)
            norm_dve(dve, ch, "ln1", XTh, XTl, XS)
            to_float(17, 2048)
            for u in range(9):
                T, (off, w) = TILE0["ffn_up"] + 2 * u, CH[u % 3]
                if u == 3:
                    to_float(18, 2048)
                if u == 6:
                    to_float(19, 3072)
                dve.wait_ge(mm_done, T + 2)
                dve.wait_ge(sg_ready, u + 1)
                h, hh = hf[u % 2][:, 0:w], HTh[:, u // 3, off:off + w]
                stt(h, ps[:, (T + 1) % 4, 0:w], 1.0 / (127.0 * XS), sg[u % 2][:, 0:w],
                    ALU.mult, ALU.mult).then_inc(evac, 2)
                dve.wait_ge(evac, T + 2)
                ch.link(v.tensor_copy(hh, h))
                v.tensor_tensor(HTl[:, u // 3, off:off + w], h, hh, ALU.subtract).then_inc(h_done, 1)
            T = TILE0["ffn_down"]
            whole_nodes(T, T, 512, 2, lambda T, b, k, c: add_to_x(dve, T, b, k, slice(c * 512, (c + 1) * 512),
                                                                  1.0 / 127.0))
            dve.wait_ge(evac, TILE0["gnn1"])
            norm_dve(dve, ch, "ln2", XTh, XTl, XS)
            dve.wait_ge(sq_done, NT)
            dve.wait_ge(l_loaded, 48 - 16)
            v.tensor_scalar(ssq[:, :], ssq[:, :], 1.0 / DIM, 1e-6, ALU.mult, ALU.add).then_inc(ms_ready, 1)
            dve.wait_ge(ms_root, 1)
            ch.link(v.tensor_scalar(rn[:, 0], ssq[:, :], 1.0 / (XS * WS), None, ALU.mult))
            v.tensor_scalar(rn[:, 1], ssq[:, :], HS / (XS * WS), None, ALU.mult).then_inc(rn_ready, 1)
            for r in range(NREL):
                ch.link(v.memset(Hh[r][:, :, FF:FFP], 0.0))
                v.memset(Hh[r][:, :, FF:FF + 1], 1.0)
                ch.link(v.memset(Hl[r][:, :, FF:FFP], 0.0))
            ch.link(v.memset(y[:, :, FF:FFP], 0.0))
            T0 = TILE0["gnn1"]
            for i in range(NT):
                T = T0 + i
                dve.wait_ge(mm_done, T + 1)
                stt(y[:, i, 0:FF], ps[0:TN, T % 4, 0:FF], rn[:, 0, i:i + 1], cbias, ALU.mult,
                    ALU.add).then_inc(evac, 1)
            for r in range(NREL):
                for i in range(NT):
                    T = T0 + (r + 1) * NT + i
                    dve.wait_ge(h_hi, r * NT + i + 1)
                    stt(Hl[r][:, i, 0:FF], ps[0:TN, T % 4, 0:FF], rn[:, 1, i:i + 1], Hh[r][:, i, 0:FF],
                        ALU.mult, ALU.subtract).then_inc(evac, 1)
            dve.wait_ge(evac, T0 + 3 * NT)
            v.engine_nop().then_inc(h_done, 2 * NT)

            def low(u, r):
                dve.wait_ge(c_hi, u + 1)
                v.tensor_tensor(Bl[r], Bi[r], Bh[r], ALU.subtract).then_inc(c_lo, 1)

            def mean_add(q, r, c0):
                for l in range(2):
                    t = 3 * NT + 2 * r + l
                    T, b = q * 4 + (T0 + t), (T0 + t) % 4
                    dve.wait_ge(mm_done, T + 1)
                    o = ps[0:TN, b]
                    ch.link(v.tensor_scalar(dens[:, 0:1], o[:, FF:FF + 1], 1.0, HS, ALU.max, ALU.mult))
                    ch.link(v.reciprocal(dens[:, 1:2], dens[:, 0:1]))
                    dve.wait_ge(evac, T)
                    yy = row(y, q * 2 + l)[:, 0:FF]
                    stt(yy, o[:, 0:FF], dens[:, 1:2], yy, ALU.mult, ALU.add).then_inc(evac, 1)
            low(0, 0)
            with dve.Fori(0, NT // 2 - 1) as q:
                ch.enter(q, 8)
                low(q * 2 + 1, 1)
                mean_add(q, 0, 0)
                low(q * 2 + 2, 0)
                mean_add(q, 1, 0)
            ch.leave(NT // 2 - 1)
            low(NT - 1, 1)
            mean_add(NT // 2 - 1, 0, 0)
            mean_add(NT // 2 - 1, 1, 0)
            dve.wait_ge(evac, T0 + 5 * NT)
            v.tensor_scalar(ye, y, 0.0, None, ALU.min).then_inc(y_min, 1)
            ch.link(v.tensor_scalar(y, y, 0.0, None, ALU.max))
            dve.wait_ge(y_exp, 1)
            stt(y, ye, -1.0, y, ALU.add, ALU.add).then_inc(y_done, 1)
            for i in range(NT):
                dve.wait_ge(turn_hi, H0["gnn1"] + i + 1)
                at = slice(i * TN, (i + 1) * TN)
                stt(yTl[0:FB, :, at], turn_view(i % 2, 3, FB), YS, yTh[0:FB, :, at], ALU.mult,
                    ALU.subtract).then_inc(turn_lo, 1)
            T = TILE0["gnn1_out"]
            dve.wait_ge(zx_added, NT)
            whole_nodes(T, T, 512, 2, lambda T, b, k, c: add_to_x(dve, T, b, k, slice(c * 512, (c + 1) * 512),
                                                                  1.0 / (YS * WS)))
            dve.wait_ge(turn_hi, H0["gnn1"] + NT)
            for s in range(2):
                ch.link(v.memset(vf[s][:, :, 128:129], 1.0))

            def first1(p, T, b, s):
                for t in range(13):
                    e = (s + t) % 2
                    E = p * 13 + t
                    bank = ps[:, (b + t) % 4]
                    if t < 3:
                        off, w = CH[t]
                        o, vw = qf[s][:, off:off + w], (lambda a: a[:, 0:w])
                    else:
                        o, vw = kf[s][:, t - 3], (lambda a: a[0:TN, 0:128])
                    dve.wait_ge(e_relu, E + 1)
                    if t >= 3:
                        v.tensor_scalar(vf[s][:, t - 3, 0:128], bank[0:TN, 128:256], 1.0 / (XS * WS), None,
                                        ALU.mult)
                    v.tensor_scalar(vw(er[2 + e]), vw(bank), 1.0 / (XS * WS), 0.0, ALU.mult,
                                    ALU.min).then_inc(evac, 1)
                    dve.wait_ge(e_exp, E + 1)
                    v.tensor_tensor(o, vw(er[e]), vw(er[2 + e]), ALU.add).then_inc(k_done, 1)

            def second1(p, T, b, s):
                dve.wait_ge(kv_done, p + 1)
                kv = pt[:, 0, s]
                for h in range(2):
                    rows = slice(h * DH, (h + 1) * DH)
                    v.tensor_copy(kvs[rows, s, h * DH:(h + 1) * DH], kv[rows, h * DH:(h + 1) * DH])
                    q = v.tensor_copy(kvs[rows, s, 128 + h:129 + h], kv[rows, 128:129])
                q.then_inc(kv_out, 1)
                for a in range(5):
                    dve.wait_ge(mm_done, T + (a + 1))
                    dve.wait_ge(evac, T + a)
                    o = ps[0:TN, (b + a) % 4, 0:260].rearrange("p (l n) -> p l n", l=2)
                    dd = dens[:, :].rearrange("p (l h) -> p l h", l=2)
                    ch.link(v.tensor_scalar(dd, o[:, :, 128:130], 1e-6, None, ALU.add))
                    ch.link(v.reciprocal(dens[:, :], dens[:, :]))
                    v.tensor_tensor(O1[:, 2 * a:2 * a + 2, bass.ds(p * 128, 128)]
                                    .rearrange("p l (h d) -> p l h d", h=2),
                                    o[:, :, 0:128].rearrange("p l (h d) -> p l h d", h=2),
                                    dd.unsqueeze(3).to_broadcast([TN, 2, 2, DH]), ALU.mult).then_inc(evac, 1)

            pairs1(dve, first1, second1, ch, 20)
            piped(lambda i, s: None, lambda i, s: turn_lows(dve, "tO", i, s, XTh, XTl, OS1), dve)
            for i in range(4):
                for k in range(NT):
                    if i == 0:
                        dve.wait_ge(x_biased, NT + k + 1)
                    T = TILE0["mix1_out"] + NT * i + k
                    add_to_x(dve, T, T, k, slice(i * 256, (i + 1) * 256), 1.0 / (OS1 * WS))
            dve.wait_ge(evac, TILE0["gate"])
            norm_dve(dve, ch, "ln3", XTh, XTl, XS)
            dve.wait_ge(gate_w, 64)
            ch.link(v.tensor_scalar(wg_h, wg_f, WS, None, ALU.mult))
            stt(wg_l, wg_f, WS, wg_h, ALU.mult, ALU.subtract).then_inc(gate_split, 1)
            T = TILE0["gate"]

            def wide(a):
                return a.unsqueeze(2).to_broadcast([TN, NT, NE])

            revs = gid.unsqueeze(1).to_broadcast([TN, NT, NE])
            dve.wait_ge(mm_done, T + 1)
            v.tensor_scalar(gs[0], ps[0:TN, T % 4, 0:NT * NE].rearrange("p (i e) -> p i e", e=NE),
                            1.0 / (XS * WS), None, ALU.mult).then_inc(evac, 1)
            dve.wait_ge(evac, T + 1)
            ch.link(v.tensor_reduce(g1[0], gs[0], AX.X, ALU.max))
            v.tensor_tensor(gs[1], gs[0], wide(g1[0]), ALU.subtract).then_inc(g_mask, 1)
            dve.wait_ge(g_exp, 1)
            ch.link(v.tensor_reduce(g1[1], gs[2], AX.X, ALU.add))
            ch.link(v.reciprocal(g1[1], g1[1]))
            ch.link(v.tensor_tensor(gs[3], gs[2], wide(g1[1]), ALU.mult))

            def pick(p, o):
                ch.link(v.tensor_reduce(g1[0], p, AX.X, ALU.max))
                ch.link(v.tensor_tensor(gs[4], p, wide(g1[0]), ALU.is_equal))
                ch.link(v.tensor_tensor(gs[4], gs[4], revs, ALU.mult))
                ch.link(v.tensor_reduce(g1[0], gs[4], AX.X, ALU.max))
                ch.link(v.tensor_tensor(o, gs[4], wide(g1[0]), ALU.is_equal))
            pick(gs[3], gs[6])
            ch.link(stt(gs[1], gs[6], -2.0, gs[3], ALU.mult, ALU.add))
            pick(gs[1], gs[7])
            ch.link(v.tensor_tensor(gs[6], gs[6], gs[7], ALU.add))
            ch.link(v.tensor_tensor(gs[3], gs[3], gs[6], ALU.mult))
            ch.link(v.tensor_reduce(g1[1], gs[3], AX.X, ALU.add))
            ch.link(v.reciprocal(g1[1], g1[1]))
            ch.link(v.tensor_tensor(gs[5], gs[3], wide(g1[1]), ALU.mult))
            v.tensor_scalar(gs[6], gs[5], 1.0 / WS, None, ALU.mult).then_inc(scores_ready, 1)
            dve.wait_ge(scores_ready, 1)

            def up(eng, e, T, s, b=None):
                b = T if b is None else b
                for h in range(2):
                    for c, (off, w) in enumerate(CH):
                        t = 3 * h + c
                        m = mr[t % 2][:, 0:w]
                        dve.wait_ge(m_hi, e * 6 + (t + 1))
                        v.tensor_scalar(m, ps[:, (b + t) % 4, 0:w], 1.0 / (XS * WS), b1t[:, h, bass.ds(e, 1)],
                                        ALU.mult, ALU.add).then_inc(evac, 1)
                        dve.wait_ge(evac, T + (t + 1))
                        stt(MHl[s][:, h, off:off + w], m, 0.0, MHh[s][:, h, off:off + w],
                            ALU.max, ALU.subtract).then_inc(m_done, 1)

            def down(eng, e, T, s, b):
                for i in range(NT):
                    for c in range(2):
                        t = 2 * i + c
                        x = X[:, i, c * 512:(c + 1) * 512]
                        dve.wait_ge(mm_done, T + (t + 1))
                        dve.wait_ge(evac, T + (t - 3))
                        stt(x, ps[0:TN, (b + t) % 4, :], gs[6][:, i, bass.ds(e, 1)], x,
                            ALU.mult, ALU.add).then_inc(evac, 1)
            up(dve, 0, MT0, 0)
            for a in range(3):
                t, w = TILE0["gate"] + 7 + a, (500, 500, 250)[a]
                dve.wait_ge(mm_done, t + 1)
                v.tensor_copy(scT[:, 500 * a:500 * a + w], ps[0:NE, t % 4, 0:w]).then_inc(evac, 1)
            T = TILE0["gate"] + 10
            whole_nodes(T, T, 512, 2, lambda T, b, k, c: add_to_x(dve, T, b, k, slice(c * 512, (c + 1) * 512), 1.0))
            experts(dve, up, down)


_INS = ["x", "src", "dst", "edge_type_2", "L0_gnn_b", "L0_mix_gamma", "L0_mix_beta", "L0_mix_b_out",
        "L1_gnn_conv_bias", "L1_mix_b_out", "L1_ffn_Wg", "L1_ffn_b2"]


def lay_out(inputs):
    a = {n: np.ascontiguousarray(inputs[n]) for n in _INS}

    def kp(w):
        w = np.asarray(w)
        return w.reshape(w.shape[0] // 128, 128, -1).transpose(1, 0, 2)

    def chunks(w, n):
        w = kp(w)
        return np.ascontiguousarray(np.stack([w[:, :, i:i + n].reshape(128, -1) for i in range(0, w.shape[2], n)]))

    def pairs(w):
        w = kp(w).reshape(128, KD, 3, PAIRS, 128)
        return np.ascontiguousarray(w.transpose(3, 0, 1, 2, 4).reshape(PAIRS, 128, -1))

    a["w_mix0"] = pairs(inputs["L0_mix_W_qkv"])
    a["w_out0"] = chunks(inputs["L0_mix_W_out"], 256)
    a["w_gnn0"] = chunks(np.asarray(inputs["L0_gnn_W"]).T, 256)
    gate, up = (kp(np.asarray(inputs[n]).T).reshape(128, KD, 3, 128) for n in ("L0_ffn_w_gate", "L0_ffn_w_up"))
    a["w_up0"] = np.ascontiguousarray(np.stack([gate, up], 3).transpose(2, 0, 1, 3, 4).reshape(3, 128, -1))
    a["w_down0"] = np.ascontiguousarray(kp(np.asarray(inputs["L0_ffn_w_down"]).T).reshape(1, 128, -1))
    rel = np.asarray(inputs["L1_gnn_W_rel"])
    a["w_gnn1"] = np.ascontiguousarray(np.stack([kp(w).reshape(128, -1) for w in
                                                 (inputs["L1_gnn_W_root"], rel[0], rel[1])]))
    wo = np.asarray(inputs["L1_gnn_wo_weight"])
    a["w_gnn1_out"] = np.ascontiguousarray(np.pad(wo, ((0, FFP - FF), (0, 0))).reshape(3, FB, DIM)
                                           .transpose(1, 0, 2).reshape(FB, 3 * DIM))
    a["w_mix1"] = pairs(np.asarray(inputs["L1_mix_w_qkv"]).T)
    a["w_out1"] = chunks(np.asarray(inputs["L1_mix_w_out"]).T, 256)
    w1 = [kp(w).reshape(128, -1) for w in np.asarray(inputs["L1_ffn_W1"])]
    w2 = [kp(w).reshape(128, -1) for w in np.asarray(inputs["L1_ffn_W2"])]
    order = [w1[0]]
    for e in range(NE - 1):
        order += [w1[e + 1], w2[e]]
    a["w_moe"] = np.ascontiguousarray(np.stack(order + [w2[NE - 1]]))
    a["b1"] = np.ascontiguousarray(np.asarray(inputs["L1_ffn_b1"]).reshape(NE, 2, 128).transpose(2, 1, 0))
    a["ln_weight"] = np.ascontiguousarray(np.asarray(inputs["L1_gnn_ln_weight"]).reshape(KD, 128).T)
    a["rev"] = np.arange(NE, 0, -1, dtype=np.float32)
    return a


def kernel(**inputs):
    import concourse.bacc as bacc
    from concourse.bass_utils import run_bass_kernel_spmd
    arrays = lay_out(inputs)
    nc = bacc.Bacc("TRN2", target_bir_lowering=False, num_devices=1)
    A = {n: nc.dram_tensor(f"in_{n}", v.shape, mybir.dt.from_np(v.dtype), kind="ExternalInput").ap()
         for n, v in arrays.items()}
    out = nc.dram_tensor("out_0", (NODES, DIM), F32, kind="ExternalOutput").ap()
    build_program(nc, A, out)
    r = run_bass_kernel_spmd(nc, [{f"in_{n}": v for n, v in arrays.items()}], core_ids=[0])
    return r.results[0]["out_0"]
```
